# Optimizing a Trainium2 kernel written in Bass

```python
import numpy as np
import jax
import jax.numpy as jnp

def _softmax(x, axis=-1):
    return jax.nn.softmax(x, axis=axis)

def _gelu(x):
    return jax.nn.gelu(x, approximate=True)

def _silu(x):
    return jax.nn.silu(x)

def _sigmoid(x):
    return jax.nn.sigmoid(x)

def _layernorm(x, axis=-1, eps=1e-05):
    m = jnp.mean(x, axis=axis, keepdims=True)
    v = jnp.var(x, axis=axis, keepdims=True)
    return (x - m) / jnp.sqrt(v + eps)

def _scatter_add(tgt, idx, src, axis=0):
    return tgt.at[idx].add(src)

def _segment_sum(src, seg, n):
    return jax.ops.segment_sum(src, seg, n)
kernel_name = 'mk_audio_tower_d2_tok_audfeat1024_r4_b1efff'

def setup_inputs(seed: int=0):
    np.random.seed(seed)
    _w = jnp.asarray

    def _rec_inputs():
        import jax
        import jax.numpy as jnp
        _rk = jax.random.key(seed)
        x = -0.000494162 + 1.00033 * jax.random.normal(jax.random.fold_in(_rk, 1), (64, 1, 750), jnp.float32)
        return x
    x = _rec_inputs()

    def _L0_tok_setup():
        import jax, jax.numpy as jnp
        import numpy as np
        from jax import lax
        B, C_IN, L = (8, 1, 120000)
        DIMS, HEAD = (256, 16)
        HEAD_DIM = DIMS // HEAD
        GROUPS = DIMS // 8

        def _conv1d(x, w, b, stride, pad, groups=1):
            y = lax.conv_general_dilated(x, w, window_strides=(stride,), padding=[(pad, pad)], dimension_numbers=('NCH', 'OIH', 'NCH'), feature_group_count=groups)
            return y + b[None, :, None]

        def _gelu(v):
            return jax.nn.gelu(v, approximate=False)
        key = jax.random.key(seed)
        ks = jax.random.split(key, 12)
        s = 0.02
        inp = {'x': jax.random.normal(ks[0], (B, C_IN, L), dtype=jnp.float32), 'w1': jax.random.normal(ks[1], (DIMS // 8, C_IN, 15), dtype=jnp.float32) * s, 'b1': jnp.zeros((DIMS // 8,), dtype=jnp.float32), 'w2': jax.random.normal(ks[2], (DIMS // 4, DIMS // 8, 7), dtype=jnp.float32) * s, 'b2': jnp.zeros((DIMS // 4,), dtype=jnp.float32), 'w3': jax.random.normal(ks[3], (DIMS, DIMS // 4, 9), dtype=jnp.float32) * s, 'b3': jnp.zeros((DIMS,), dtype=jnp.float32), 'w4': jax.random.normal(ks[4], (DIMS, DIMS // GROUPS, 3), dtype=jnp.float32) * s, 'b4': jnp.zeros((DIMS,), dtype=jnp.float32), 'w5': jax.random.normal(ks[5], (DIMS, DIMS, 1), dtype=jnp.float32) * s, 'b5': jnp.zeros((DIMS,), dtype=jnp.float32), 'rope_freqs': 1.0 / 50.0 ** (jnp.arange(0, HEAD_DIM, 2, dtype=jnp.float32) / HEAD_DIM), 'norm_w': jnp.ones((DIMS,), dtype=jnp.float32)}
        return inp
    _L0_tok_all = _L0_tok_setup()
    _L0_tok_in = {k: v for k, v in _L0_tok_all.items() if k in ('w1', 'b1', 'w2', 'b2', 'w3', 'b3', 'w4', 'b4', 'w5', 'b5', 'rope_freqs', 'norm_w')}
    del _L0_tok_all

    def _L0_attn_setup():
        import jax, jax.numpy as jnp
        import numpy as np
        B, N, D, H = (2, 512, 256, 8)
        DH = D // H
        key = jax.random.key(seed)
        k0, k1, k2 = jax.random.split(key, 3)
        s = 1.0 / np.sqrt(D).astype(np.float32)
        return {'x': jax.random.normal(k0, (B, N, D), dtype=jnp.float32), 'w_qkv': jax.random.normal(k1, (3 * D, D), dtype=jnp.float32) * s, 'b_qkv': jnp.zeros((3 * D,), dtype=jnp.float32), 'w_o': jax.random.normal(k2, (D, D), dtype=jnp.float32) * s, 'b_o': jnp.zeros((D,), dtype=jnp.float32)}
    _L0_attn_all = _L0_attn_setup()
    _L0_attn_in = {k: v for k, v in _L0_attn_all.items() if k in ('w_qkv', 'b_qkv', 'w_o', 'b_o')}
    del _L0_attn_all

    def _L0_ffn_setup():
        import jax, jax.numpy as jnp
        import numpy as np
        B, S, D_MODEL, D_HIDDEN = (4, 512, 256, 1024)

        def act_quant(x):
            scale = 127.0 / jnp.clip(jnp.max(jnp.abs(x), axis=-1, keepdims=True), 1e-05)
            return jnp.clip(jnp.round(x * scale), -128, 127) / scale

        def weight_quant(w):
            scale = 1.0 / jnp.clip(jnp.mean(jnp.abs(w)), 1e-05)
            return jnp.clip(jnp.round(w * scale), -1, 1) / scale

        def bit_linear(x, w):
            xq = x + jax.lax.stop_gradient(act_quant(x) - x)
            wq = w + jax.lax.stop_gradient(weight_quant(w) - w)
            return jnp.einsum('bsd,hd->bsh', xq, wq)

        def depthwise_conv1d(x_bcl, w, b):
            y = jax.lax.conv_general_dilated(x_bcl, w, window_strides=(1,), padding=[(1, 1)], dimension_numbers=('NCH', 'OIH', 'NCH'), feature_group_count=x_bcl.shape[1])
            return y + b[None, :, None]
        key = jax.random.key(seed)
        ks = jax.random.split(key, 5)
        lim1 = 1.0 / np.sqrt(D_MODEL)
        lim2 = 1.0 / np.sqrt(D_HIDDEN)
        limc = 1.0 / np.sqrt(3.0)
        return {'x': jax.random.normal(ks[0], (B, S, D_MODEL), dtype=jnp.float32), 'w1': jax.random.uniform(ks[1], (D_HIDDEN, D_MODEL), jnp.float32, -lim1, lim1), 'conv_w': jax.random.uniform(ks[2], (D_HIDDEN, 1, 3), jnp.float32, -limc, limc), 'conv_b': jax.random.uniform(ks[3], (D_HIDDEN,), jnp.float32, -limc, limc), 'w2': jax.random.uniform(ks[4], (D_MODEL, D_HIDDEN), jnp.float32, -lim2, lim2)}
    _L0_ffn_all = _L0_ffn_setup()
    _L0_ffn_in = {k: v for k, v in _L0_ffn_all.items() if k in ('w1', 'conv_w', 'conv_b', 'w2')}
    del _L0_ffn_all

    def _L1_attn_setup():
        import jax, jax.numpy as jnp
        import numpy as np
        INDIM = 256
        NHEADS = 16
        DK = INDIM // NHEADS
        DV = INDIM // NHEADS
        B, S = (4, 512)
        key = jax.random.key(seed)
        ks = jax.random.split(key, 5)
        x = jax.random.normal(ks[0], (B, S, INDIM), dtype=jnp.float32)
        std_qk = np.sqrt(2.0 / (INDIM + DK)).astype(np.float32)
        std_v = np.sqrt(2.0 / (INDIM + DV)).astype(np.float32)
        Wq = jax.random.normal(ks[1], (NHEADS * DK, INDIM), dtype=jnp.float32) * std_qk
        Wk = jax.random.normal(ks[2], (NHEADS * DK, INDIM), dtype=jnp.float32) * std_qk
        Wv = jax.random.normal(ks[3], (NHEADS * DV, INDIM), dtype=jnp.float32) * std_v
        std_o = np.sqrt(2.0 / (NHEADS * DV + INDIM)).astype(np.float32)
        Wo = jax.random.normal(ks[4], (INDIM, NHEADS * DV), dtype=jnp.float32) * std_o
        bq = jnp.zeros((NHEADS * DK,), jnp.float32)
        bk = jnp.zeros((NHEADS * DK,), jnp.float32)
        bv = jnp.zeros((NHEADS * DV,), jnp.float32)
        bo = jnp.zeros((INDIM,), jnp.float32)
        return {'x': x, 'Wq': Wq, 'bq': bq, 'Wk': Wk, 'bk': bk, 'Wv': Wv, 'bv': bv, 'Wo': Wo, 'bo': bo}
    _L1_attn_all = _L1_attn_setup()
    _L1_attn_in = {k: v for k, v in _L1_attn_all.items() if k in ('Wq', 'bq', 'Wk', 'bk', 'Wv', 'bv', 'Wo', 'bo')}
    del _L1_attn_all

    def _L1_ffn_setup():
        import jax, jax.numpy as jnp
        import numpy as np
        B, S, H, NH, E, F = (4, 256, 256, 16, 8, 1024)
        D = H // NH
        EPS = 1e-05

        def _layernorm(x, g, b):
            mu = jnp.mean(x, axis=-1, keepdims=True)
            var = jnp.var(x, axis=-1, keepdims=True)
            return (x - mu) * jax.lax.rsqrt(var + EPS) * g + b
        key = jax.random.key(seed)
        ks = jax.random.split(key, 16)
        s = 0.02
        return {'x': jax.random.normal(ks[0], (B, S, H), jnp.float32), 'ln1_g': jnp.ones((H,), jnp.float32), 'ln1_b': jnp.zeros((H,), jnp.float32), 'ln2_g': jnp.ones((H,), jnp.float32), 'ln2_b': jnp.zeros((H,), jnp.float32), 'wq': jax.random.normal(ks[1], (H, H), jnp.float32) * s, 'bq': jnp.zeros((H,), jnp.float32), 'wk': jax.random.normal(ks[2], (H, H), jnp.float32) * s, 'bk': jnp.zeros((H,), jnp.float32), 'wv': jax.random.normal(ks[3], (H, H), jnp.float32) * s, 'bv': jnp.zeros((H,), jnp.float32), 'wo': jax.random.normal(ks[4], (H, H), jnp.float32) * s, 'bo': jnp.zeros((H,), jnp.float32), 'gate_w': jax.random.normal(ks[5], (H, E), jnp.float32) * s, 'gate_b': jnp.zeros((E,), jnp.float32), 'w1': jax.random.normal(ks[6], (E, H, F), jnp.float32) * s, 'b1': jnp.zeros((E, F), jnp.float32), 'w2': jax.random.normal(ks[7], (E, F, H), jnp.float32) * s, 'b2': jnp.zeros((E, H), jnp.float32)}
    _L1_ffn_all = _L1_ffn_setup()
    _L1_ffn_in = {k: v for k, v in _L1_ffn_all.items() if k in ('ln1_g', 'ln1_b', 'ln2_g', 'ln2_b', 'wq', 'bq', 'wk', 'bk', 'wv', 'bv', 'wo', 'bo', 'gate_w', 'gate_b', 'w1', 'b1', 'w2', 'b2')}
    del _L1_ffn_all
    return {'x': x, 'L0_tok_w1': _L0_tok_in['w1'], 'L0_tok_b1': _L0_tok_in['b1'], 'L0_tok_w2': _L0_tok_in['w2'], 'L0_tok_b2': _L0_tok_in['b2'], 'L0_tok_w3': _L0_tok_in['w3'], 'L0_tok_b3': _L0_tok_in['b3'], 'L0_tok_w4': _L0_tok_in['w4'], 'L0_tok_b4': _L0_tok_in['b4'], 'L0_tok_w5': _L0_tok_in['w5'], 'L0_tok_b5': _L0_tok_in['b5'], 'L0_tok_rope_freqs': _L0_tok_in['rope_freqs'], 'L0_tok_norm_w': _L0_tok_in['norm_w'], 'L0_attn_w_qkv': _L0_attn_in['w_qkv'], 'L0_attn_b_qkv': _L0_attn_in['b_qkv'], 'L0_attn_w_o': _L0_attn_in['w_o'], 'L0_attn_b_o': _L0_attn_in['b_o'], 'L0_ffn_w1': _L0_ffn_in['w1'], 'L0_ffn_conv_w': _L0_ffn_in['conv_w'], 'L0_ffn_conv_b': _L0_ffn_in['conv_b'], 'L0_ffn_w2': _L0_ffn_in['w2'], 'L1_attn_Wq': _L1_attn_in['Wq'], 'L1_attn_bq': _L1_attn_in['bq'], 'L1_attn_Wk': _L1_attn_in['Wk'], 'L1_attn_bk': _L1_attn_in['bk'], 'L1_attn_Wv': _L1_attn_in['Wv'], 'L1_attn_bv': _L1_attn_in['bv'], 'L1_attn_Wo': _L1_attn_in['Wo'], 'L1_attn_bo': _L1_attn_in['bo'], 'L1_ffn_ln1_g': _L1_ffn_in['ln1_g'], 'L1_ffn_ln1_b': _L1_ffn_in['ln1_b'], 'L1_ffn_ln2_g': _L1_ffn_in['ln2_g'], 'L1_ffn_ln2_b': _L1_ffn_in['ln2_b'], 'L1_ffn_wq': _L1_ffn_in['wq'], 'L1_ffn_bq': _L1_ffn_in['bq'], 'L1_ffn_wk': _L1_ffn_in['wk'], 'L1_ffn_bk': _L1_ffn_in['bk'], 'L1_ffn_wv': _L1_ffn_in['wv'], 'L1_ffn_bv': _L1_ffn_in['bv'], 'L1_ffn_wo': _L1_ffn_in['wo'], 'L1_ffn_bo': _L1_ffn_in['bo'], 'L1_ffn_gate_w': _L1_ffn_in['gate_w'], 'L1_ffn_gate_b': _L1_ffn_in['gate_b'], 'L1_ffn_w1': _L1_ffn_in['w1'], 'L1_ffn_b1': _L1_ffn_in['b1'], 'L1_ffn_w2': _L1_ffn_in['w2'], 'L1_ffn_b2': _L1_ffn_in['b2']}

def reference(x, L0_tok_w1, L0_tok_b1, L0_tok_w2, L0_tok_b2, L0_tok_w3, L0_tok_b3, L0_tok_w4, L0_tok_b4, L0_tok_w5, L0_tok_b5, L0_tok_rope_freqs, L0_tok_norm_w, L0_attn_w_qkv, L0_attn_b_qkv, L0_attn_w_o, L0_attn_b_o, L0_ffn_w1, L0_ffn_conv_w, L0_ffn_conv_b, L0_ffn_w2, L1_attn_Wq, L1_attn_bq, L1_attn_Wk, L1_attn_bk, L1_attn_Wv, L1_attn_bv, L1_attn_Wo, L1_attn_bo, L1_ffn_ln1_g, L1_ffn_ln1_b, L1_ffn_ln2_g, L1_ffn_ln2_b, L1_ffn_wq, L1_ffn_bq, L1_ffn_wk, L1_ffn_bk, L1_ffn_wv, L1_ffn_bv, L1_ffn_wo, L1_ffn_bo, L1_ffn_gate_w, L1_ffn_gate_b, L1_ffn_w1, L1_ffn_b1, L1_ffn_w2, L1_ffn_b2):
    import jax
    import jax.numpy as jnp

    def _L0_tok_ref(x, w1, b1, w2, b2, w3, b3, w4, b4, w5, b5, rope_freqs, norm_w):
        import jax, jax.numpy as jnp
        import numpy as np
        from jax import lax
        B, C_IN, L = (8, 1, 120000)
        DIMS, HEAD = (256, 16)
        HEAD_DIM = DIMS // HEAD
        GROUPS = DIMS // 8

        def _conv1d(x, w, b, stride, pad, groups=1):
            y = lax.conv_general_dilated(x, w, window_strides=(stride,), padding=[(pad, pad)], dimension_numbers=('NCH', 'OIH', 'NCH'), feature_group_count=groups)
            return y + b[None, :, None]

        def _gelu(v):
            return jax.nn.gelu(v, approximate=False)
        h = _gelu(_conv1d(x, w1, b1, stride=8, pad=7))
        h = _gelu(_conv1d(h, w2, b2, stride=4, pad=3))
        h = _gelu(_conv1d(h, w3, b3, stride=5, pad=4))
        h = _gelu(_conv1d(h, w4, b4, stride=1, pad=1, groups=GROUPS))
        h = _gelu(_conv1d(h, w5, b5, stride=1, pad=0))
        h = jnp.transpose(h, (0, 2, 1))
        Bb, T, D = h.shape
        xh = h.reshape(Bb, T, HEAD, HEAD_DIM).transpose(0, 2, 1, 3)
        t = jnp.arange(T, dtype=jnp.float32)
        ang = t[:, None] * rope_freqs[None, :]
        cos, sin = (jnp.cos(ang), jnp.sin(ang))
        xp = xh.reshape(Bb, HEAD, T, HEAD_DIM // 2, 2)
        xr, xi = (xp[..., 0], xp[..., 1])
        out_r = xr * cos - xi * sin
        out_i = xr * sin + xi * cos
        xh = jnp.stack([out_r, out_i], axis=-1).reshape(Bb, HEAD, T, HEAD_DIM)
        h = xh.transpose(0, 2, 1, 3).reshape(Bb, T, D)
        ms = jnp.mean(h * h, axis=-1, keepdims=True)
        return h * jax.lax.rsqrt(ms + 1e-08) * norm_w

    def _L0_attn_ref(x, w_qkv, b_qkv, w_o, b_o):
        import jax, jax.numpy as jnp
        import numpy as np
        B, N, D, H = (2, 512, 256, 8)
        DH = D // H
        b, n, d = x.shape
        h = H
        dh = d // h
        qkv = x @ w_qkv.T + b_qkv
        qkv = qkv.reshape(b, n, 3, dh, h)
        qkv = jnp.transpose(qkv, (2, 0, 4, 1, 3))
        q, k, v = (qkv[0], qkv[1], qkv[2])
        attn = jnp.einsum('bhik,bhjk->bhij', q, k)
        out = jnp.einsum('bhik,bhkj->bhij', attn, v)
        out = jnp.transpose(out, (0, 2, 1, 3)).reshape(b, n, d)
        return out @ w_o.T + b_o

    def _L0_ffn_ref(x, w1, conv_w, conv_b, w2):
        import jax, jax.numpy as jnp
        import numpy as np
        B, S, D_MODEL, D_HIDDEN = (4, 512, 256, 1024)

        def act_quant(x):
            scale = 127.0 / jnp.clip(jnp.max(jnp.abs(x), axis=-1, keepdims=True), 1e-05)
            return jnp.clip(jnp.round(x * scale), -128, 127) / scale

        def weight_quant(w):
            scale = 1.0 / jnp.clip(jnp.mean(jnp.abs(w)), 1e-05)
            return jnp.clip(jnp.round(w * scale), -1, 1) / scale

        def bit_linear(x, w):
            xq = x + jax.lax.stop_gradient(act_quant(x) - x)
            wq = w + jax.lax.stop_gradient(weight_quant(w) - w)
            return jnp.einsum('bsd,hd->bsh', xq, wq)

        def depthwise_conv1d(x_bcl, w, b):
            y = jax.lax.conv_general_dilated(x_bcl, w, window_strides=(1,), padding=[(1, 1)], dimension_numbers=('NCH', 'OIH', 'NCH'), feature_group_count=x_bcl.shape[1])
            return y + b[None, :, None]
        h = bit_linear(x, w1)
        h = depthwise_conv1d(h.transpose(0, 2, 1), conv_w, conv_b)
        h = h.transpose(0, 2, 1)
        h = jax.nn.silu(h)
        return bit_linear(h, w2)

    def _L1_attn_ref(x, Wq, bq, Wk, bk, Wv, bv, Wo, bo):
        import jax, jax.numpy as jnp
        import numpy as np
        INDIM = 256
        NHEADS = 16
        DK = INDIM // NHEADS
        DV = INDIM // NHEADS
        B, S = (4, 512)
        b, s, _ = x.shape
        q = (x @ Wq.T + bq).reshape(b, s, NHEADS, DK)
        k = (x @ Wk.T + bk).reshape(b, s, NHEADS, DK)
        v = (x @ Wv.T + bv).reshape(b, s, NHEADS, DV)
        w = jnp.einsum('bshd,bzhd->bhsz', q, k)
        w = w / jnp.sqrt(jnp.float32(DV))
        w = jax.nn.softmax(w, axis=-1)
        vw = jnp.einsum('bhsz,bzhd->bshd', w, v)
        vw = vw.reshape(b, s, NHEADS * DV)
        out = vw @ Wo.T + bo
        return out

    def _L1_ffn_ref(x, ln1_g, ln1_b, ln2_g, ln2_b, wq, bq, wk, bk, wv, bv, wo, bo, gate_w, gate_b, w1, b1, w2, b2):
        import jax, jax.numpy as jnp
        import numpy as np
        B, S, H, NH, E, F = (4, 256, 256, 16, 8, 1024)
        D = H // NH
        EPS = 1e-05

        def _layernorm(x, g, b):
            mu = jnp.mean(x, axis=-1, keepdims=True)
            var = jnp.var(x, axis=-1, keepdims=True)
            return (x - mu) * jax.lax.rsqrt(var + EPS) * g + b
        b, s, h = x.shape
        hn = _layernorm(x, ln1_g, ln1_b)
        q = (hn @ wq + bq).reshape(b, s, NH, D).transpose(0, 2, 1, 3)
        k = (hn @ wk + bk).reshape(b, s, NH, D).transpose(0, 2, 1, 3)
        v = (hn @ wv + bv).reshape(b, s, NH, D).transpose(0, 2, 1, 3)
        scores = jnp.einsum('bhqd,bhkd->bhqk', q, k) / jnp.sqrt(jnp.float32(D))
        attn = jax.nn.softmax(scores, axis=-1)
        o = jnp.einsum('bhqk,bhkd->bhqd', attn, v)
        o = o.transpose(0, 2, 1, 3).reshape(b, s, h)
        x = x + (o @ wo + bo)
        hn2 = _layernorm(x, ln2_g, ln2_b).reshape(-1, h)
        logits = hn2 @ gate_w + gate_b
        idx = jnp.argmax(logits, axis=-1)
        mid = jax.nn.relu(jnp.einsum('th,ehf->etf', hn2, w1) + b1[:, None, :])
        y = jnp.einsum('etf,efh->eth', mid, w2) + b2[:, None, :]
        moe = y[idx, jnp.arange(hn2.shape[0])]
        return x + moe.reshape(b, s, h)
    h = _L0_tok_ref(x, L0_tok_w1, L0_tok_b1, L0_tok_w2, L0_tok_b2, L0_tok_w3, L0_tok_b3, L0_tok_w4, L0_tok_b4, L0_tok_w5, L0_tok_b5, L0_tok_rope_freqs, L0_tok_norm_w)
    h = h + _L0_attn_ref(_layernorm(h, axis=-1), L0_attn_w_qkv, L0_attn_b_qkv, L0_attn_w_o, L0_attn_b_o)
    h = h + _L0_ffn_ref(_layernorm(h, axis=-1), L0_ffn_w1, L0_ffn_conv_w, L0_ffn_conv_b, L0_ffn_w2)
    h = h + _L1_attn_ref(_layernorm(h, axis=-1), L1_attn_Wq, L1_attn_bq, L1_attn_Wk, L1_attn_bk, L1_attn_Wv, L1_attn_bv, L1_attn_Wo, L1_attn_bo)
    h = h + _L1_ffn_ref(_layernorm(h, axis=-1), L1_ffn_ln1_g, L1_ffn_ln1_b, L1_ffn_ln2_g, L1_ffn_ln2_b, L1_ffn_wq, L1_ffn_bq, L1_ffn_wk, L1_ffn_bk, L1_ffn_wv, L1_ffn_bv, L1_ffn_wo, L1_ffn_bo, L1_ffn_gate_w, L1_ffn_gate_b, L1_ffn_w1, L1_ffn_b1, L1_ffn_w2, L1_ffn_b2)
    return h

_drawn_inputs = setup_inputs


def setup_inputs(seed=0):
    import zlib

    import numpy as np

    out = dict(_drawn_inputs(seed))
    spreads = {'L0_tok_b1': (0.0, 0.8),
     'L0_tok_b2': (0.0, 0.8),
     'L0_tok_b3': (0.0, 0.729),
     'L0_tok_b4': (0.0, 0.1),
     'L0_tok_b5': (0.0, 0.1),
     'L0_tok_norm_w': (1.0, 0.2),
     'L0_attn_b_qkv': (0.0, 0.1),
     'L0_attn_b_o': (0.0, 0.8),
     'L1_attn_bq': (0.0, 0.8),
     'L1_attn_bk': (0.0, 2.0),
     'L1_attn_bv': (0.0, 0.8),
     'L1_attn_bo': (0.0, 0.8),
     'L1_ffn_ln1_g': (1.0, 0.6),
     'L1_ffn_ln1_b': (0.0, 0.8),
     'L1_ffn_ln2_g': (1.0, 0.6),
     'L1_ffn_ln2_b': (0.0, 0.8),
     'L1_ffn_bq': (0.0, 0.8),
     'L1_ffn_bk': (0.0, 2.0),
     'L1_ffn_bv': (0.0, 0.8),
     'L1_ffn_bo': (0.0, 0.8),
     'L1_ffn_gate_b': (0.0, 0.8),
     'L1_ffn_b1': (0.0, 0.8),
     'L1_ffn_b2': (0.0, 2.0)}
    factors = {'x': 8.0,
     'L0_tok_w1': 8.0,
     'L0_tok_w2': 8.0,
     'L0_tok_w3': 8.0,
     'L0_tok_w4': 4.445,
     'L0_ffn_w1': 8.0,
     'L0_ffn_conv_w': 8.0,
     'L0_ffn_conv_b': 8.0,
     'L0_ffn_w2': 8.0,
     'L1_attn_Wq': 4.753,
     'L1_attn_Wk': 4.652,
     'L1_ffn_wq': 8.0,
     'L1_ffn_wk': 8.0,
     'L1_ffn_wv': 8.0,
     'L1_ffn_wo': 8.0,
     'L1_ffn_gate_w': 7.872,
     'L1_ffn_w1': 8.0,
     'L1_ffn_w2': 8.0}
    for name, (base, spread) in spreads.items():
        noise = np.random.default_rng([zlib.crc32(name.encode()), seed]).standard_normal(out[name].shape)
        drawn = base * np.exp(spread * noise) if base else spread * noise
        out[name] = jnp.asarray(drawn.astype(out[name].dtype))
    for name, factor in factors.items():
        out[name] = (out[name] * factor).astype(out[name].dtype)
    return out
```

```python
from contextlib import ExitStack

import numpy as np

import concourse.bass as bass
from concourse import mybir

F32 = mybir.dt.float32
BF16 = mybir.dt.bfloat16
ALU = mybir.AluOpType
ACT = mybir.ActivationFunctionType
AX = mybir.AxisListType

P = 128
B, L = 64, 750
T = 5
D = 256
KC = D // P
NT = 4
BT = B // NT
R = BT * T
N = B * T
C1, K1, S1 = 32, 15, 8
C2, K2, S2 = 64, 7, 4
K3, S3 = 9, 5
TM = P // C1
NG, NJ = 8, 3
WIN = NJ * TM * S1
L1, L2 = 94, 24
HA, DA = 8, 32
HB, DB = 16, 16
FF = 1024
FG = FF // P
E = 8
RING = 3
ROUND = 12582912.0
BIG = 1e30
PI = float(np.pi)
TURN = [6.28125]
TURN.append(float((np.float32(2 * np.pi - TURN[0]).view(np.uint32) & np.uint32(0xFFFFF000)).view(np.float32)))
TURN.append(float(np.float32(2 * np.pi - TURN[0] - TURN[1])))

COLS = [("b1", 1), ("b2", 1), ("b3", 2), ("b4", 2), ("bq0", 2), ("bk0", 2), ("cw", 24), ("cb", 8),
        ("bq1", 2), ("bk1", 2), ("g1", 2), ("h1", 2), ("bq2", 2), ("bk2", 2), ("g2", 2), ("h2", 2),
        ("eb1", 64)]
ROWS = [("b5", D), ("nw", D), ("bv0", D), ("bo0", D), ("bv1", D), ("bo1", D), ("bv2", D), ("bo2", D),
        ("gb", E), ("fr", 8)]
CONST = [("ident", P), ("same", R), ("ohq", R), ("ohk", NT * R), ("par", 2), ("tpos", 1), ("rank", E)]


def places(table):
    at, out = 0, {}
    for name, n in table:
        out[name] = (at, n)
        at += n
    return out, at


COL, NCOL = places(COLS)
ROW, NROW = places(ROWS)
CON, NCON = places(CONST)


def tower(nc, a, out):
    with ExitStack() as ctx:
        def sb(name, shape, dt=F32):
            return ctx.enter_context(nc.sbuf_tensor(name, shape, dt))

        sems = {}

        def S(name):
            if name not in sems:
                sems[name] = ctx.enter_context(nc.semaphore(name))
            return sems[name]

        ps = ctx.enter_context(nc.psum_tensor("ps", [P, 8, 512], F32))

        xw = sb("xw", [P, NG, B])
        w1 = sb("w1", [P, NJ, P])
        w2 = sb("w2", [P, 2, P])
        w3 = sb("w3", [P, 5, D])
        w4 = sb("w4", [P, KC, 3, P])
        w5 = sb("w5", [P, KC, D])
        wqkv0 = sb("wqkv0", [P, KC, 3 * D])
        wo0 = sb("wo0", [P, KC, D])
        f1 = sb("f1", [P, KC * FF])
        f2 = sb("f2", [P, FG * D])
        fq = sb("fq", [P, 2 * KC * FF], BF16)
        f1q, f2q = fq[:, 0:KC * FF], fq[:, KC * FF:]
        wA = sb("wA", [P, KC, 4 * D])
        wB = sb("wB", [P, KC, 4 * D])
        gw = sb("gw", [P, KC, E])
        ring1 = sb("ring1", [P, RING, KC, FF])
        ring2 = sb("ring2", [P, RING, FG, D])
        eb2 = sb("eb2", [E, D])
        cols = sb("cols", [P, NCOL])
        rows = sb("rows", [R, NROW])
        con = sb("con", [P, NCON])
        identb = sb("identb", [P, P], BF16)
        ones = sb("ones", [P, P])
        onesb = sb("onesb", [P, P], BF16)
        ohb = sb("ohb", [P, R + NT * R], BF16)

        def col(name, i=0, p=slice(None)):
            at = COL[name][0] + i
            return cols[p, at:at + 1]

        def row(name):
            at, n = ROW[name]
            return rows[:, at:at + n]

        def cst(name, p=slice(None)):
            at, n = CON[name]
            return con[p, at:at + n]

        ident = cst("ident")

        ARENA = max(78 * B, 2 * FG * N)
        arena = sb("arena", [P, ARENA])
        H1 = arena[:, 0:25 * B].rearrange("p (u b) -> p u b", b=B)
        H2 = arena[:, 25 * B:54 * B].rearrange("p (u b) -> p u b", b=B)
        H3 = arena[:, 54 * B:68 * B].rearrange("p (m u b) -> p m u b", m=KC, b=B)
        H4 = arena[:, 68 * B:78 * B].rearrange("p (m n) -> p m n", m=KC)
        SC = NT * NT * R
        prob = [arena[0:R, i * SC:(i + 1) * SC] for i in range(2)]
        probT = [arena[0:R, (2 + i) * SC:(3 + i) * SC] for i in range(2)]
        hid = arena[:, 0:FG * N].rearrange("p (g n) -> p g n", g=FG)
        hidc = arena[:, FG * N:2 * FG * N].rearrange("p (g n) -> p g n", g=FG)

        X = sb("X", [R, NT, D])
        Y = sb("Y", [R, NT, D])
        Z = sb("Z", [R, NT, D])
        Zq = sb("Zq", [R, NT, D], BF16)
        ZT = sb("ZT", [P, KC, N])
        ZqT = sb("ZqT", [P, KC, N], BF16)
        QT = sb("QT", [P, KC, N])
        KT = sb("KT", [P, KC, 2, N])
        V = sb("V", [R, NT, HB, DB + 1])
        V0 = sb("V0", [R, NT, D])
        O = sb("O", [R, NT, D])
        OT = sb("OT", [P, KC, N])
        hq = sb("hq", [P, FG, N], BF16)
        mx1 = sb("mx1", [P, N])
        bc = sb("bc", [P, N])
        diag = sb("diag", [R, NT, R])
        st = sb("st", [R, NT, 6])
        mv = sb("mv", [R, NT, 2])
        ve = sb("ve", [R, NT])
        sd = sb("sd", [R, NT])
        rs = sb("rs", [R, NT])
        rt = sb("rt", [R, NT])
        amax = sb("amax", [R, NT])
        qs = sb("qs", [R, NT])
        iv = sb("iv", [R, NT])
        smax = sb("smax", [R, HB])
        rsum = sb("rsum", [R, 2, HB])
        parb = sb("parb", [P, 2, KC, 2])
        ang = sb("ang", [R, 2, 8])
        trn = sb("trn", [R, 2, 8])
        cs = sb("cs", [R, 2, 8])
        wsum = sb("wsum", [P, 2])
        wsc = sb("wsc", [P, 2])
        wiv = sb("wiv", [P, 2])
        cwq = sb("cwq", [P, 24])
        lg = sb("lg", [R, NT, E])
        lm = sb("lm", [R, NT])
        oh = sb("oh", [R, NT, E])
        ohT = sb("ohT", [E, N])
        dmask = fq[0:R, 0:E * N].rearrange("p (e i n) -> p e i n", e=E, i=NT)
        mask = arena[:, 0:E * N].rearrange("p (e n) -> p e n", e=E)
        MID = 4
        mid = arena[:, E * N:(E + MID) * N].rearrange("p (e n) -> p e n", e=MID)
        yT = arena[:, (E + MID) * N:(E + MID + KC) * N].rearrange("p (e n) -> p e n", e=KC)
        bvv = [sb(f"bvv{li}", [R, 2 * HB, DB]) for li in range(2)]
        FFB = [3, 4, 5, 6, 7, 3, 4, 5]

        block = ctx.enter_context(nc.Block())

        @block.sync
        def _(sp):
            def load(dst, name, sem):
                sp.dma_start(dst, a[name]).then_inc(S(sem), 16)

            load(xw[:], "xw", "ld_x")
            load(w1[:], "w1", "ld_x")
            load(cols[:], "cols", "ld_cols")
            load(con[:], "con", "ld_con")
            load(w2[:], "w2", "ld_w2")
            load(w3[:], "w3", "ld_w3")
            load(w4[:], "w4", "ld_w4")
            load(w5[:], "w5", "ld_w5")
            sp.dma_start(rows[:], a["rows"].partition_broadcast(R)).then_inc(S("ld_rows"), 16)
            load(f1[:], "f1", "ld_f1")
            load(wqkv0[:], "wqkv0", "ld_qkv0")
            load(wo0[:], "wo0", "ld_wo0")
            load(f2[:], "f2", "ld_f2")
            load(wA[:], "wA", "ld_wA")
            load(wB[:], "wB", "ld_wB")
            load(gw[:], "gw", "ld_gw")
            load(eb2[:], "eb2", "ld_gw")
            for e in range(E):
                if e >= RING:
                    sp.wait_ge(S("mid_used"), (e - RING + 1) * FG)
                sp.dma_start(ring1[:, e % RING], a["e1"][e]).then_inc(S(f"ld_e{e % RING}"), 16)
                sp.dma_start(ring2[:, e % RING], a["e2"][e]).then_inc(S(f"ld_e{e % RING}"), 16)
            o = out.rearrange("(i b) t d -> (b t) i d", i=NT)
            for i in range(NT):
                sp.wait_ge(S("out_ready"), i + 1)
                sp.dma_start(o[:, i, :], Y[:, i, :]).then_inc(S("stored"), 16)
            sp.wait_ge(S("stored"), 16 * NT)

        @block.gpsimd
        def _(pool):
            n = [0]

            def step(ins):
                n[0] += 1
                ins.then_inc(S("pool_steps"), 1)

            def settle():
                pool.wait_ge(S("pool_steps"), n[0])

            for dst, done in ((H1[:, 0, :], None), (H1[64:128, 24, :], "h1_zeros"), (H2[0:64, 0:4, :], None),
                              (H2[0:64, 28, :], None), (H2[64:128, 0:3, :], None),
                              (H2[64:128, 27:29, :], None), (H3[:, :, 0, :], None), (H3[:, :, 6, :], "h3_zeros")):
                step(nc.gpsimd.memset(dst, 0.0))
                settle()
                if done:
                    pool.sem_inc(S(done), 1)
            nc.gpsimd.memset(ones[:], 1.0)
            nc.gpsimd.memset(onesb[:], 1.0)
            step(nc.gpsimd.memset(V[:, :, :, DB:DB + 1], 1.0))
            settle()
            pool.sem_inc(S("ones"), 1)
            for w, (src, dst) in enumerate(((f1, f1q), (f2, f2q))):
                pool.wait_ge(S("w_scale"), w + 1)
                step(nc.gpsimd.tensor_scalar(src[:], src[:], wsc[:, w:w + 1], ROUND, ALU.mult, ALU.add))
                settle()
                step(nc.gpsimd.tensor_scalar(src[:], src[:], ROUND, 1.0, ALU.subtract, ALU.min))
                settle()
                nc.gpsimd.tensor_scalar(dst[:], src[:], -1.0, None, ALU.max).then_inc(S("w_ternary"), 1)

        @block.scalar
        def _(act):
            def copy_out(dst, src):
                return nc.scalar.activation(dst, src, ACT.Identity)

            act.wait_ge(S("angles"), 1)
            nc.scalar.activation(cs[:], ang[:], ACT.Sin).then_inc(S("sincos"), 1)
            act.wait_ge(S("ld_cols"), 16)
            act.wait_ge(S("h1_zeros"), 1)
            for j in range(NJ):
                act.wait_ge(S("conv1"), j + 1)
                src = ps[:, j, :].rearrange("p (g b) -> p g b", b=B)
                if j < NJ - 1:
                    nc.scalar.activation(H1[:, 1 + j:23 + j:3, :], src, ACT.Gelu,
                                         bias=col("b1")).then_inc(S("h1"), 1)
                else:
                    nc.scalar.activation(H1[:, 3:22:3, :], src[:, 0:7, :], ACT.Gelu, bias=col("b1"))
                    nc.scalar.activation(H1[0:64, 24, :], src[0:64, 7, :], ACT.Gelu,
                                         bias=col("b1", 0, slice(0, 64))).then_inc(S("h1"), 1)
            act.wait_ge(S("h3_zeros"), 1)
            for q in range(3):
                act.wait_ge(S("conv2"), q + 1)
                src = ps[:, 3 + q, :].rearrange("p (u b) -> p u b", b=B)
                nc.scalar.activation(H2[0:64, 4 + 8 * q:12 + 8 * q, :], src[0:64], ACT.Gelu,
                                     bias=col("b2", 0, slice(0, 64)))
                nc.scalar.activation(H2[64:128, 3 + 8 * q:11 + 8 * q, :], src[64:128], ACT.Gelu,
                                     bias=col("b2", 0, slice(64, 128))).then_inc(S("h2"), 1)
            for m in range(KC):
                act.wait_ge(S("conv3"), m + 1)
                nc.scalar.activation(H3[:, m, 1:6, :], ps[:, 6 + m, 0:N].rearrange("p (t b) -> p t b", b=B),
                                     ACT.Gelu, bias=col("b3", m)).then_inc(S("h3"), 1)
            for m in range(KC):
                act.wait_ge(S("conv4"), m + 1)
                nc.scalar.activation(H4[:, m, :].rearrange("p (b t) -> p t b", t=T),
                                     ps[:, m, 0:N].rearrange("p (t b) -> p t b", b=B),
                                     ACT.Gelu, bias=col("b4", m)).then_inc(S("h4"), 1)
            for h in range(2):
                act.wait_ge(S("conv5_biased"), h + 1)
                nc.scalar.activation(Y[:, 2 * h:2 * h + 2, :], Y[:, 2 * h:2 * h + 2, :],
                                     ACT.Gelu).then_inc(S("h5"), 1)
            act.wait_ge(S("ld_f1"), 16)
            nc.scalar.activation(f1q[:], f1[:], ACT.Abs, accum_out=wsum[:, 0:1])
            act.wait_ge(S("ld_f2"), 16)
            nc.scalar.activation(f2q[:], f2[:], ACT.Abs, accum_out=wsum[:, 1:2]).then_inc(S("w_sums"), 1)

            act.wait_ge(S("roped"), 1)
            for i in range(NT):
                ins = nc.scalar.activation(V0[:, i, :], Z[:, i, :], ACT.Square, accum_out=ve[:, i:i + 1])
            ins.then_inc(S("squares"), 1)

            def root(tag):
                act.wait_ge(S(tag + "_var"), 1)
                nc.scalar.activation(sd[:], ve[:], ACT.Sqrt).then_inc(S(tag + "_root"), 1)

            def half_T(tag, affine=None):
                act.wait_ge(S(tag + "_turned"), 1)
                if affine:
                    nc.scalar.activation(ZT[:, 0, :], ps[:, 0, 0:N], ACT.Identity, bias=col(affine[1], 0),
                                         scale=col(affine[0], 0)).then_inc(S(tag + "_T"), 1)
                else:
                    copy_out(ZT[:, 0, :], ps[:, 0, 0:N]).then_inc(S(tag + "_T"), 1)

            root("rms")
            root("ln0")
            half_T("ln0")
            for m in range(KC):
                act.wait_ge(S("q0"), m + 1)
                nc.scalar.activation(QT[:, m, :], ps[:, 2 + m, 0:N], ACT.Identity,
                                     bias=col("bq0", m)).then_inc(S("q0_T"), 1)
            act.wait_ge(S("out0"), 1)
            copy_out(OT[:, 0, :], ps[:, 0, 0:N]).then_inc(S("out0_T"), 1)

            root("ln1")
            act.wait_ge(S("zq_turned"), 1)
            copy_out(ZqT[:, 0, :], ps[:, 0, :].bitcast(BF16)[:, 0:N]).then_inc(S("zq_T"), 1)
            for g in range(FG):
                act.wait_ge(S("hid_scaled"), g + 1)
                nc.scalar.activation(hidc[:, g, :], hid[:, g, :], ACT.Identity, bias=col("cb", g),
                                     scale=cwq[:, 3 * g + 1:3 * g + 2]).then_inc(S("tap1"), 1)
            for g in range(FG):
                act.wait_ge(S("conv_done"), g + 1)
                nc.scalar.activation(hid[:, g, :], hidc[:, g, :], ACT.Silu).then_inc(S("silu"), 1)

            def softmax_attention(tag):
                for m in range(KC):
                    act.wait_ge(S(tag + "_q"), m + 1)
                    nc.scalar.activation(QT[:, m, :], ps[:, 2 + m, 0:N], ACT.Identity,
                                         bias=col("bq" + tag[-1], m)).then_inc(S(tag + "_q_T"), 1)

                def exps(i):
                    act.wait_ge(S(tag + "_less"), i + 1)
                    nc.scalar.activation(prob[i % 2], prob[i % 2], ACT.Exp,
                                         scale=DB ** -0.5).then_inc(S(tag + "_exp"), 1)

                def turned(i):
                    act.wait_ge(S(tag + "_ptr"), i + 1)
                    if i >= 2:
                        act.wait_ge(S(tag + "_av"), i - 1)
                    copy_out(probT[i % 2].rearrange("p (k n) -> p k n", k=4)[:, 0:3, :],
                             ps[0:R, 4 * (i % 2):4 * (i % 2) + 3, 0:4 * R]).then_inc(S(tag + "_pT"), 1)
                    copy_out(probT[i % 2].rearrange("p (k n) -> p k n", k=4)[:, 3, :],
                             ps[0:R, 4 * (i % 2) + 3, 0:4 * R]).then_inc(S(tag + "_pT"), 1)

                exps(0)
                for i in range(NT):
                    if i + 1 < NT:
                        exps(i + 1)
                    turned(i)
                act.wait_ge(S(tag + "_oturned"), 1)
                copy_out(OT[:, 0, :], ps[:, 0, 0:N]).then_inc(S(tag + "_o_T"), 1)

            root("ln2")
            half_T("ln2")
            softmax_attention("att1")
            root("pre")
            root("ln3")
            half_T("ln3", ("g1", "h1"))
            softmax_attention("att2")
            root("ln4")
            half_T("ln4", ("g2", "h2"))

            act.wait_ge(S("oh_turned"), 1)
            copy_out(ohT[:], ps[0:E, 3, 0:N]).then_inc(S("oh_T"), 1)
            for e in range(0, E, 2):
                act.wait_ge(S("mask_bc"), e + 1)
                copy_out(mask[:, e, :], ps[:, 4 + e % 4, 0:N]).then_inc(S("mask_a"), 1)
            for u in range(E * FG):
                act.wait_ge(S("mid_raw"), u + 1)
                if u >= MID:
                    act.wait_ge(S("mid_used"), u - MID + 1)
                nc.scalar.activation(mid[:, u % MID, :], ps[:, u % 4, 0:N], ACT.Relu,
                                     bias=col("eb1", u)).then_inc(S("mid_relu"), 1)
            act.wait_ge(S("moe"), 1)
            copy_out(yT[:, 0, :], ps[:, 6, 0:N]).then_inc(S("moe_T"), 1)

        @block.vector
        def _(dve):
            n = [0]

            def step(ins):
                n[0] += 1
                ins.then_inc(S("dve_steps"), 1)

            def settle():
                dve.wait_ge(S("dve_steps"), n[0])

            V_ = nc.vector
            dve.wait_ge(S("ld_con"), 16)
            V_.tensor_copy(identb[:], ident).then_inc(S("const_bf"), 1)
            V_.tensor_copy(ohb[:, 0:R], cst("ohq")).then_inc(S("const_bf"), 1)
            V_.tensor_copy(ohb[:, R:], cst("ohk")).then_inc(S("const_bf"), 1)
            dve.wait_ge(S("ld_rows"), 16)
            for s in range(2):
                step(V_.tensor_scalar(ang[:, s, :], row("fr"), cst("tpos", slice(0, R)), None, ALU.mult))
            settle()
            step(V_.tensor_scalar(trn[:, 0, :], ang[:, 0, :], 1.0 / (2 * PI), 0.25, ALU.mult, ALU.add))
            step(V_.tensor_scalar(trn[:, 1, :], ang[:, 1, :], 1.0 / (2 * PI), None, ALU.mult))
            settle()
            step(V_.tensor_scalar(trn[:], trn[:], ROUND, None, ALU.add))
            settle()
            step(V_.tensor_scalar(trn[:], trn[:], ROUND, None, ALU.subtract))
            settle()
            for c in TURN:
                step(V_.scalar_tensor_tensor(out=ang[:], in0=trn[:], scalar=-c, in1=ang[:],
                                             op0=ALU.mult, op1=ALU.add))
                settle()
            step(V_.tensor_scalar(ang[:, 0, :], ang[:, 0, :], PI / 2, None, ALU.add))
            settle()
            V_.tensor_scalar(ang[:], ang[:], 3.1415925, -3.1415925, ALU.min, ALU.max).then_inc(S("angles"), 1)

            dve.wait_ge(S("ld_cols"), 16)
            for li, nm in enumerate(("bk1", "bk2")):
                for m in range(KC):
                    step(V_.tensor_scalar(parb[:, li, m, :], cst("par"), col(nm, m), None, ALU.mult))

            b5 = row("b5").unsqueeze(1).to_broadcast([R, 2, D])
            for h in range(2):
                dve.wait_ge(S("conv5"), h + 1)
                V_.tensor_tensor(Y[:, 2 * h:2 * h + 2, :], ps[0:R, 2 + h, :].rearrange("p (i d) -> p i d", i=2),
                                 b5, ALU.add).then_inc(S("conv5_biased"), 1)
            dve.wait_ge(S("sincos"), 1)
            dve.wait_ge(S("h5"), 2)
            yv = Y[:].rearrange("p i (h k c) -> p (i h) k c", h=HB, c=2)
            zv = Z[:].rearrange("p i (h k c) -> p (i h) k c", h=HB, c=2)
            cosb = cs[:, 0, :].unsqueeze(1).to_broadcast([R, NT * HB, 8])
            sinb = cs[:, 1, :].unsqueeze(1).to_broadcast([R, NT * HB, 8])
            t0 = O[:].rearrange("p i d -> p (i d)")[:, 0:512].rearrange("p (h k) -> p h k", k=8)
            t1 = O[:].rearrange("p i d -> p (i d)")[:, 512:1024].rearrange("p (h k) -> p h k", k=8)
            step(V_.tensor_tensor(t0, yv[:, :, :, 1], sinb, ALU.mult))
            step(V_.tensor_tensor(t1, yv[:, :, :, 1], cosb, ALU.mult))
            step(V_.tensor_tensor(zv[:, :, :, 0], yv[:, :, :, 0], cosb, ALU.mult))
            step(V_.tensor_tensor(zv[:, :, :, 1], yv[:, :, :, 0], sinb, ALU.mult))
            settle()
            step(V_.tensor_tensor(zv[:, :, :, 0], zv[:, :, :, 0], t0, ALU.subtract))
            V_.tensor_tensor(zv[:, :, :, 1], zv[:, :, :, 1], t1, ALU.add).then_inc(S("roped"), 1)

            def inverse_root(tag):
                dve.wait_ge(S(tag + "_root"), 1)
                step(V_.reciprocal(rs[:], sd[:]))
                settle()
                step(V_.tensor_tensor(rt[:], rs[:], rs[:], ALU.mult))
                settle()
                step(V_.tensor_tensor(rt[:], rt[:], ve[:], ALU.mult))
                settle()
                step(V_.tensor_scalar(rt[:], rt[:], -0.5, 1.5, ALU.mult, ALU.add))
                settle()
                step(V_.tensor_tensor(rs[:], rs[:], rt[:], ALU.mult))
                settle()

            dve.wait_ge(S("w_total"), 1)
            step(V_.tensor_scalar(wiv[:], ps[:, 4, 0:2], 1.0 / (FF * D), 1e-5, ALU.mult, ALU.max))
            settle()
            step(V_.reciprocal(wsc[:], wiv[:]))
            settle()
            V_.tensor_scalar(cwq[:], cols[:, COL["cw"][0]:COL["cw"][0] + 24], wiv[:, 0:1], None,
                             ALU.mult).then_inc(S("w_scale"), 2)

            dve.wait_ge(S("squares"), 1)
            V_.tensor_scalar(ve[:], ve[:], 1.0 / D, 1e-8, ALU.mult, ALU.add).then_inc(S("rms_var"), 1)
            inverse_root("rms")
            for i in range(NT):
                step(V_.scalar_tensor_tensor(out=X[:, i, :], in0=Z[:, i, :], scalar=rs[:, i:i + 1],
                                             in1=row("nw"), op0=ALU.mult, op1=ALU.mult))
            settle()

            def layernorm(tag, bias=None, dst=Z):
                for i in range(NT):
                    step(V_.bn_stats(st[:, i, :], X[:, i, :]))
                settle()
                for i in range(NT):
                    step(V_.bn_aggr(mv[:, i, :], st[:, i, :]))
                settle()
                V_.tensor_scalar(ve[:], mv[:, :, 1], 1e-5, None, ALU.add).then_inc(S(tag + "_var"), 1)
                dve.wait_ge(S(tag + "_var"), 1)
                inverse_root(tag)
                for i in range(NT):
                    V_.tensor_scalar(dst[:, i, :], X[:, i, :], mv[:, i, 0:1], rs[:, i:i + 1],
                                     ALU.subtract, ALU.mult).then_inc(S(tag + "_z"), 1)
                if bias:
                    dve.wait_ge(S(tag + "_z"), NT)
                    step(V_.tensor_tensor(X[:], X[:], row(bias).unsqueeze(1).to_broadcast([R, NT, D]), ALU.add))
                    settle()

            def half_T(tag, affine=None):
                dve.wait_ge(S(tag + "_turned"), 2)
                if affine:
                    V_.tensor_scalar(ZT[:, 1, :], ps[:, 1, 0:N], col(affine[0], 1), col(affine[1], 1),
                                     ALU.mult, ALU.add).then_inc(S(tag + "_T"), 1)
                else:
                    V_.tensor_copy(ZT[:, 1, :], ps[:, 1, 0:N]).then_inc(S(tag + "_T"), 1)

            def add_out(sem, banks, nxt):
                for h in range(2):
                    dve.wait_ge(S(sem), h + 1)
                    step(V_.tensor_tensor(X[:, 2 * h:2 * h + 2, :],
                                          ps[0:R, banks + h, :].rearrange("p (i d) -> p i d", i=2),
                                          X[:, 2 * h:2 * h + 2, :], ALU.add))
                settle()

            layernorm("ln0", "bo0")
            half_T("ln0")
            for m in range(KC):
                dve.wait_ge(S("k0"), m + 1)
                V_.tensor_scalar(KT[:, m, 0, :], ps[:, 4 + m, 0:N], col("bk0", m), None,
                                 ALU.add).then_inc(S("k0_T"), 1)
            for h in range(2):
                dve.wait_ge(S("v0"), h + 1)
                V_.tensor_tensor(V0[:, 2 * h:2 * h + 2, :], ps[0:R, 6 + h, :].rearrange("p (i d) -> p i d", i=2),
                                 row("bv0").unsqueeze(1).to_broadcast([R, 2, D]),
                                 ALU.add).then_inc(S("v0_sb"), 1)
            for c in range(2):
                dve.wait_ge(S("s0"), c + 1)
                V_.tensor_tensor(prob[c].rearrange("p (k u q) -> p k u q", k=4, u=4),
                                 ps[0:R, 4 * c:4 * c + 4, 0:4 * R].rearrange("p k (u q) -> p k u q", u=4),
                                 cst("same", slice(0, R)).unsqueeze(1).unsqueeze(1).to_broadcast([R, 4, 4, R]),
                                 ALU.mult).then_inc(S("s0_sb"), 1)
            dve.wait_ge(S("out0"), 2)
            V_.tensor_copy(OT[:, 1, :], ps[:, 1, 0:N]).then_inc(S("out0_T"), 1)
            add_out("o0", 2, None)

            def act_scale(tag):
                step(V_.tensor_scalar(amax[:], amax[:], 1e-5, None, ALU.max))
                settle()
                step(V_.reciprocal(qs[:], amax[:]))
                step(V_.tensor_scalar(iv[:], amax[:], 1.0 / 127.0, None, ALU.mult))
                settle()
                step(V_.tensor_scalar(qs[:], qs[:], 127.0, None, ALU.mult))
                settle()

            def diagonal(sc, tag):
                V_.tensor_tensor(diag[:], ident[0:R, 0:R].unsqueeze(1).to_broadcast([R, NT, R]),
                                 sc[:].unsqueeze(2).to_broadcast([R, NT, R]), ALU.mult).then_inc(S(tag), 1)

            layernorm("ln1")
            dve.wait_ge(S("ln1_z"), NT)
            step(V_.tensor_reduce(amax[:], Z[:], AX.X, ALU.max, apply_absolute_value=True))
            settle()
            act_scale("zq")
            for i in range(NT):
                step(V_.tensor_scalar(Z[:, i, :], Z[:, i, :], qs[:, i:i + 1], ROUND, ALU.mult, ALU.add))
            settle()
            step(V_.tensor_scalar(Z[:], Z[:], ROUND, 127.0, ALU.subtract, ALU.min))
            settle()
            V_.tensor_scalar(Zq[:], Z[:], -128.0, None, ALU.max).then_inc(S("zq"), 1)
            diagonal(iv, "iv1_diag")
            dve.wait_ge(S("zq_turned"), 2)
            V_.tensor_copy(ZqT[:, 1, :], ps[:, 1, :].bitcast(BF16)[:, 0:N]).then_inc(S("zq_T"), 1)
            dve.wait_ge(S("iv1_bc"), 1)
            step(V_.tensor_copy(bc[:], ps[:, 2, 0:N]))
            settle()
            for g in range(FG):
                dve.wait_ge(S("ff1"), g + 1)
                V_.tensor_tensor(hid[:, g, :], ps[:, FFB[g], 0:N], bc[:], ALU.mult).then_inc(S("hid_scaled"), 1)
            dve.wait_ge(S("hid_scaled"), FG)
            for g in range(FG):
                src = hid[:, g, :].rearrange("p (b t) -> p b t", t=T)
                dst = hidc[:, g, :].rearrange("p (b t) -> p b t", t=T)
                dve.wait_ge(S("tap1"), g + 1)
                step(V_.scalar_tensor_tensor(out=dst[:, :, 1:T], in0=src[:, :, 0:T - 1],
                                             scalar=cwq[:, 3 * g:3 * g + 1], in1=dst[:, :, 1:T],
                                             op0=ALU.mult, op1=ALU.add))
                settle()
                V_.scalar_tensor_tensor(out=dst[:, :, 0:T - 1], in0=src[:, :, 1:T],
                                        scalar=cwq[:, 3 * g + 2:3 * g + 3], in1=dst[:, :, 0:T - 1],
                                        op0=ALU.mult, op1=ALU.add).then_inc(S("conv_done"), 1)
            dve.wait_ge(S("silu"), FG)
            V_.tensor_reduce(mx1[:], hid[:].rearrange("p g n -> p n g"), AX.X, ALU.max,
                             apply_absolute_value=True).then_inc(S("mx1"), 1)
            dve.wait_ge(S("mx1_turned"), 1)
            step(V_.tensor_reduce(amax[:], ps[0:R, 0, :].rearrange("p (i c) -> p i c", i=NT), AX.X, ALU.max))
            settle()
            act_scale("hq")
            diagonal(qs, "qs2_diag")
            step(V_.tensor_scalar(iv[:], iv[:], wiv[0:R, 1:2], None, ALU.mult))
            dve.wait_ge(S("qs2_bc"), 1)
            step(V_.tensor_copy(bc[:], ps[:, 1, 0:N]))
            settle()
            for g in range(FG):
                step(V_.tensor_tensor(hid[:, g, :], hid[:, g, :], bc[:], ALU.mult))
            settle()
            step(V_.tensor_scalar(hid[:], hid[:], ROUND, None, ALU.add))
            settle()
            step(V_.tensor_scalar(hid[:], hid[:], ROUND, 127.0, ALU.subtract, ALU.min))
            settle()
            V_.tensor_scalar(hq[:], hid[:], -128.0, None, ALU.max).then_inc(S("hq"), 1)
            for i in range(NT):
                dve.wait_ge(S("ff2"), i // 2 + 1)
                step(V_.scalar_tensor_tensor(out=X[:, i, :], in0=ps[0:R, 2 + i // 2, (i % 2) * D:(i % 2 + 1) * D],
                                             scalar=iv[:, i:i + 1], in1=X[:, i, :],
                                             op0=ALU.mult, op1=ALU.add))
            settle()

            def softmax_attention(tag, li):
                nm = "bk1" if li == 0 else "bk2"
                for m in range(KC):
                    dve.wait_ge(S(tag + "_k"), m + 1)
                    for par in range(2):
                        ins = V_.tensor_scalar(KT[:, m, par, :], ps[:, 4 + m, 0:N], con[:, CON["par"][0] + par:CON["par"][0] + par + 1],
                                               parb[:, li, m, par:par + 1], ALU.mult, ALU.add)
                    ins.then_inc(S(tag + "_k_T"), 1)
                for h in range(2):
                    dve.wait_ge(S(tag + "_v"), h + 1)
                    V_.tensor_tensor(V[:, 2 * h:2 * h + 2, :, 0:DB].rearrange("p i h d -> p (i h) d"),
                                     ps[0:R, 6 + h, :].rearrange("p (x d) -> p x d", d=DB),
                                     bvv[li][:], ALU.add).then_inc(S(tag + "_v_sb"), 1)

                def less_max(i):
                    dve.wait_ge(S(tag + "_s"), i + 1)
                    s = ps[0:R, 4 * (i % 2):4 * (i % 2) + 4, 0:4 * R].rearrange("p k (u n) -> p k u n", u=4)
                    if i >= 1:
                        dve.wait_ge(S(tag + "_less"), i)
                    step(V_.tensor_reduce(smax[:].rearrange("p (k u) -> p k u", k=4), s, AX.X, ALU.max))
                    settle()
                    if i >= 2:
                        dve.wait_ge(S(tag + "_ptr"), i - 1)
                    V_.tensor_tensor(prob[i % 2].rearrange("p (k u n) -> p k u n", k=4, u=4), s,
                                     smax[:].rearrange("p (k u) -> p k u", k=4).unsqueeze(3).to_broadcast([R, 4, 4, R]),
                                     ALU.subtract).then_inc(S(tag + "_less"), 1)

                def normalise(i):
                    dve.wait_ge(S(tag + "_av"), i + 1)
                    av = ps[0:R, 4 * (i % 2), 0:HB * (DB + 1)].rearrange("p (h d) -> p h d", h=HB)
                    step(V_.reciprocal(rsum[:, i % 2, :], av[:, :, DB]))
                    settle()
                    V_.tensor_tensor(O[:, i, :].rearrange("p (h d) -> p h d", h=HB), av[:, :, 0:DB],
                                     rsum[:, i % 2, :].unsqueeze(2).to_broadcast([R, HB, DB]),
                                     ALU.mult).then_inc(S(tag + "_o"), 1)

                less_max(0)
                less_max(1)
                for i in range(NT):
                    normalise(i)
                    if i + 2 < NT:
                        less_max(i + 2)
                dve.wait_ge(S(tag + "_oturned"), 2)
                V_.tensor_copy(OT[:, 1, :], ps[:, 1, 0:N]).then_inc(S(tag + "_o_T"), 1)
                add_out(tag + "_wo", 2, None)

            for li in range(2):
                for h in range(2):
                    step(V_.tensor_copy(bvv[li][:].rearrange("p (i h) d -> p i (h d)", i=2)[:, h, :],
                                        row("bv%d" % (li + 1))))
            settle()

            layernorm("ln2", "bo1")
            half_T("ln2")
            softmax_attention("att1", 0)
            step(V_.tensor_copy(Y[:], X[:]))
            settle()
            layernorm("pre", dst=X)
            dve.wait_ge(S("pre_z"), NT)
            layernorm("ln3", "bo2")
            half_T("ln3", ("g1", "h1"))
            softmax_attention("att2", 1)
            step(V_.tensor_tensor(Y[:], Y[:], X[:], ALU.add))
            layernorm("ln4")
            half_T("ln4", ("g2", "h2"))

            dve.wait_ge(S("logits"), 1)
            step(V_.tensor_tensor(lg[:], ps[0:R, 2, 0:NT * E].rearrange("p (i e) -> p i e", i=NT),
                                  row("gb").unsqueeze(1).to_broadcast([R, NT, E]), ALU.add))
            settle()
            step(V_.tensor_reduce(lm[:], lg[:], AX.X, ALU.max))
            settle()
            step(V_.tensor_tensor(lg[:], lg[:], lm[:].unsqueeze(2).to_broadcast([R, NT, E]), ALU.is_equal))
            settle()
            step(V_.tensor_tensor(lg[:], lg[:], cst("rank", slice(0, R)).unsqueeze(1).to_broadcast([R, NT, E]),
                                  ALU.mult))
            settle()
            step(V_.tensor_reduce(lm[:], lg[:], AX.X, ALU.max))
            settle()
            V_.tensor_tensor(oh[:], lg[:], lm[:].unsqueeze(2).to_broadcast([R, NT, E]),
                             ALU.is_equal).then_inc(S("onehot"), 1)
            dve.wait_ge(S("onehot"), 1)
            for e in range(E):
                V_.tensor_tensor(dmask[:, e], identb[0:R, 0:R].unsqueeze(1).to_broadcast([R, NT, R]),
                                 oh[:, :, e].unsqueeze(2).to_broadcast([R, NT, R]),
                                 ALU.mult).then_inc(S("mask_diag"), 1)
            for e in range(1, E, 2):
                dve.wait_ge(S("mask_bc"), e + 1)
                V_.tensor_copy(mask[:, e, :], ps[:, 4 + e % 4, 0:N]).then_inc(S("mask_v"), 1)
            dve.wait_ge(S("mask_a"), E // 2)
            dve.wait_ge(S("mask_v"), E // 2)
            for u in range(E * FG):
                dve.wait_ge(S("mid_relu"), u + 1)
                V_.tensor_tensor(mid[:, u % MID, :], mid[:, u % MID, :], mask[:, u // FG, :],
                                 ALU.mult).then_inc(S("mid"), 1)
            dve.wait_ge(S("moe"), 2)
            V_.tensor_copy(yT[:, 1, :], ps[:, 7, 0:N]).then_inc(S("moe_T"), 1)
            for h in range(2):
                dve.wait_ge(S("moe_turned"), h + 1)
                V_.tensor_tensor(Y[:, 2 * h:2 * h + 2, :], ps[0:R, h, :].rearrange("p (i d) -> p i d", i=2),
                                 Y[:, 2 * h:2 * h + 2, :], ALU.add).then_inc(S("out_ready"), 2)

        @block.tensor
        def _(pe):
            mm = nc.tensor.matmul
            pe.wait_ge(S("ld_x"), 32)
            for j in range(NJ):
                mm(ps[:, j, :], w1[:, j, :], xw[:], start=True, stop=True).then_inc(S("conv1"), 1)
            pe.wait_ge(S("ld_w2"), 16)
            pe.wait_ge(S("h1"), NJ)
            for q in range(3):
                for s in range(2):
                    ins = mm(ps[:, 3 + q, :], w2[:, s, :], H1[:, 8 * q + s:8 * q + s + 8, :],
                             start=(s == 0), stop=(s == 1))
                ins.then_inc(S("conv2"), 1)
            pe.wait_ge(S("ld_w3"), 16)
            pe.wait_ge(S("h3_zeros"), 1)
            pe.wait_ge(S("h2"), 3)
            for m in range(KC):
                for k in range(5):
                    ins = mm(ps[:, 6 + m, 0:N], w3[:, k, m * P:(m + 1) * P], H2[:, 2 * k:2 * k + 21:S3, :],
                             start=(k == 0), stop=(k == 4))
                ins.then_inc(S("conv3"), 1)
            pe.wait_ge(S("ld_w4"), 16)
            for m in range(KC):
                pe.wait_ge(S("h3"), m + 1)
                for k in range(3):
                    ins = mm(ps[:, m, 0:N], w4[:, m, k, :], H3[:, m, k:k + T, :], start=(k == 0), stop=(k == 2))
                ins.then_inc(S("conv4"), 1)
            pe.wait_ge(S("ld_w5"), 16)
            pe.wait_ge(S("h4"), 2)

            def token_major(bank, lhs, rhs, sem, nk=KC):
                for i in range(NT):
                    for k in range(nk):
                        ins = mm(ps[0:R, bank + i // 2, (i % 2) * D:(i % 2 + 1) * D],
                                 lhs(k, i), rhs(k), start=(k == 0), stop=(k == nk - 1))
                    if i % 2:
                        ins.then_inc(S(sem), 1)

            def tile(x):
                return lambda k, i: x[:, k, i * R:(i + 1) * R]

            token_major(2, tile(H4), lambda k: w5[:, k, :], "conv5")

            pe.wait_ge(S("ones"), 1)
            pe.wait_ge(S("w_sums"), 1)
            mm(ps[:, 4, 0:2], ones[:], wsum[:], start=True, stop=True).then_inc(S("w_total"), 1)

            def turn(src, tag, wait):
                pe.wait_ge(S("ld_con"), 16)
                for k in range(KC):
                    for i in range(NT):
                        if k == 0:
                            pe.wait_ge(S(wait), i + 1)
                        ins = nc.tensor.transpose(ps[:, k, i * R:(i + 1) * R], src[:, i, k * P:(k + 1) * P],
                                                  ident[0:R, 0:R])
                    ins.then_inc(S(tag), 1)

            def project(w, at, bank, sem):
                for m in range(KC):
                    for k in range(KC):
                        ins = mm(ps[:, bank + m, 0:N], w[:, k, at + m * P:at + (m + 1) * P], ZT[:, k, :],
                                 start=(k == 0), stop=(k == 1))
                    ins.then_inc(S(sem), 1)

            turn(Z, "ln0_turned", "ln0_z")
            pe.wait_ge(S("ld_qkv0"), 16)
            pe.wait_ge(S("ln0_T"), 2)
            project(wqkv0, 0, 2, "q0")
            project(wqkv0, D, 4, "k0")
            token_major(6, tile(ZT), lambda k: wqkv0[:, k, 2 * D:3 * D], "v0")
            pe.wait_ge(S("q0_T"), 2)
            pe.wait_ge(S("k0_T"), 2)
            for c in range(2):
                if c == 1:
                    pe.wait_ge(S("v0_sb"), 2)
                for ti in range(2):
                    i = 2 * c + ti
                    for m in range(KC):
                        for h in range(4):
                            ins = mm(ps[0:R, 4 * c + h, (2 * ti + m) * R:(2 * ti + m + 1) * R],
                                     KT[32 * h:32 * h + 32, m, 0, i * R:(i + 1) * R],
                                     QT[32 * h:32 * h + 32, m, i * R:(i + 1) * R], start=True, stop=True)
                ins.then_inc(S("s0"), 1)
            pe.wait_ge(S("s0_sb"), 2)
            for m in range(KC):
                for i in range(NT):
                    for h in range(4):
                        ins = mm(ps[32 * h:32 * h + 32, m, i * R:(i + 1) * R],
                                 V0[:, i, (4 * m + h) * DA:(4 * m + h + 1) * DA],
                                 prob[i // 2][:, (4 * h + 2 * (i % 2) + m) * R:(4 * h + 2 * (i % 2) + m + 1) * R],
                                 start=True, stop=True)
                ins.then_inc(S("out0"), 1)
            pe.wait_ge(S("ld_wo0"), 16)
            pe.wait_ge(S("out0_T"), 2)
            token_major(2, tile(OT), lambda k: wo0[:, k, :], "o0")

            pe.wait_ge(S("const_bf"), 3)
            pe.wait_ge(S("zq"), 1)
            for k in range(KC):
                for i in range(NT):
                    ins = nc.tensor.transpose(ps[:, k, :].bitcast(BF16)[:, i * R:(i + 1) * R],
                                              Zq[:, i, k * P:(k + 1) * P], identb[0:R, 0:R])
                ins.then_inc(S("zq_turned"), 1)
            pe.wait_ge(S("iv1_diag"), 1)
            mm(ps[:, 2, 0:N], ones[0:R, :], diag[:], start=True, stop=True).then_inc(S("iv1_bc"), 1)
            pe.wait_ge(S("zq_T"), 2)
            pe.wait_ge(S("w_ternary"), 2)
            for g in range(FG):
                if g >= 5:
                    pe.wait_ge(S("hid_scaled"), g - 4)
                for k in range(KC):
                    ins = mm(ps[:, FFB[g], 0:N], f1q[:, k * FF + g * P:k * FF + (g + 1) * P], ZqT[:, k, :],
                             start=(k == 0), stop=(k == 1))
                ins.then_inc(S("ff1"), 1)
            pe.wait_ge(S("mx1"), 1)
            for i in range(NT):
                ins = nc.tensor.transpose(ps[0:R, 0, i * P:(i + 1) * P], mx1[:, i * R:(i + 1) * R], ident)
            ins.then_inc(S("mx1_turned"), 1)
            pe.wait_ge(S("qs2_diag"), 1)
            mm(ps[:, 1, 0:N], ones[0:R, :], diag[:], start=True, stop=True).then_inc(S("qs2_bc"), 1)
            pe.wait_ge(S("hq"), 1)
            token_major(2, tile(hq), lambda k: f2q[:, k * D:(k + 1) * D], "ff2", FG)

            def softmax_attention(tag, ln, w):
                turn(Z, ln + "_turned", ln + "_z")
                pe.wait_ge(S(ln + "_T"), 2)
                project(w, 0, 2, tag + "_q")
                project(w, D, 4, tag + "_k")
                token_major(6, tile(ZT), lambda k: w[:, k, 2 * D:3 * D], tag + "_v")
                pe.wait_ge(S(tag + "_q_T"), 2)
                pe.wait_ge(S(tag + "_k_T"), 2)

                def scores(i):
                    s = 4 * (i % 2)
                    if i == 1:
                        pe.wait_ge(S(tag + "_v_sb"), 2)
                    if i >= 2:
                        pe.wait_ge(S(tag + "_o"), i - 1)
                    for h in range(4):
                        r = slice(32 * h, 32 * h + BT)
                        mm(ps[0:R, s + h, 0:4 * R], ohb[r, 0:R], ohb[r, R:R + 4 * R], start=True, stop=True)
                    for m in range(KC):
                        for h in range(4):
                            r = slice(32 * h, 32 * h + 32)
                            ins = mm(ps[0:R, s + h, 2 * m * R:2 * (m + 1) * R], QT[r, m, i * R:(i + 1) * R],
                                     KT[r, m, :, i * R:(i + 1) * R], start=False, stop=True,
                                     skip_group_check=True)
                    ins.then_inc(S(tag + "_s"), 1)

                def values(i):
                    s = 4 * (i % 2)
                    pe.wait_ge(S(tag + "_exp"), i + 1)
                    for j in range(HB):
                        ins = nc.tensor.transpose(ps[0:R, s + j // 4, (j % 4) * R:(j % 4 + 1) * R],
                                                  prob[i % 2][:, j * R:(j + 1) * R], ident[0:R, 0:R])
                    ins.then_inc(S(tag + "_ptr"), 1)
                    pe.wait_ge(S(tag + "_pT"), 2 * (i + 1))
                    for j in range(HB):
                        h = 2 * (j // 4) + j % 2 + 8 * (j % 4 // 2)
                        ins = mm(ps[0:R, s, h * (DB + 1):(h + 1) * (DB + 1)], probT[i % 2][:, j * R:(j + 1) * R],
                                 V[:, i, h, :], start=True, stop=True)
                    ins.then_inc(S(tag + "_av"), 1)

                scores(0)
                scores(1)
                for i in range(NT):
                    values(i)
                    if i + 2 < NT:
                        scores(i + 2)
                pe.wait_ge(S(tag + "_o"), NT)
                for k in range(KC):
                    for i in range(NT):
                        ins = nc.tensor.transpose(ps[:, k, i * R:(i + 1) * R], O[:, i, k * P:(k + 1) * P],
                                                  ident[0:R, 0:R])
                    ins.then_inc(S(tag + "_oturned"), 1)
                pe.wait_ge(S(tag + "_o_T"), 2)
                token_major(2, tile(OT), lambda k: w[:, k, 3 * D:4 * D], tag + "_wo")

            pe.wait_ge(S("ld_wA"), 16)
            softmax_attention("att1", "ln2", wA)
            pe.wait_ge(S("ld_wB"), 16)
            softmax_attention("att2", "ln3", wB)

            turn(Z, "ln4_turned", "ln4_z")
            pe.wait_ge(S("ld_gw"), 32)
            pe.wait_ge(S("ln4_T"), 2)
            for i in range(NT):
                for k in range(KC):
                    ins = mm(ps[0:R, 2, i * E:(i + 1) * E], ZT[:, k, i * R:(i + 1) * R], gw[:, k, :],
                             start=(k == 0), stop=(k == 1))
            ins.then_inc(S("logits"), 1)
            pe.wait_ge(S("onehot"), 1)
            for i in range(NT):
                ins = nc.tensor.transpose(ps[0:E, 3, i * R:(i + 1) * R], oh[:, i, :], ident[0:R, 0:R])
            ins.then_inc(S("oh_turned"), 1)
            for e in range(E):
                pe.wait_ge(S("mask_diag"), e + 1)
                if e >= 4:
                    pe.wait_ge(S("mask_a" if e % 2 == 0 else "mask_v"), (e - 4) // 2 + 1)
                mm(ps[:, 4 + e % 4, 0:N], onesb[0:R, :], dmask[:, e], start=True, stop=True).then_inc(S("mask_bc"), 1)
            pe.wait_ge(S("oh_T"), 1)
            pe.wait_ge(S("mask_a"), E // 2)
            pe.wait_ge(S("mask_v"), E // 2)
            for m in range(KC):
                mm(ps[:, 6 + m, 0:N], eb2[:, m * P:(m + 1) * P], ohT[:], start=True, stop=True)
            LAG = 2
            for u in range(E * FG + LAG):
                if u < E * FG:
                    e, g = u // FG, u % FG
                    if g == 0:
                        pe.wait_ge(S(f"ld_e{e % RING}"), 32 * (e // RING + 1))
                    if u >= 4:
                        pe.wait_ge(S("mid_relu"), u - 3)
                    for k in range(KC):
                        ins = mm(ps[:, u % 4, 0:N], ring1[:, e % RING, k, g * P:(g + 1) * P], ZT[:, k, :],
                                 start=(k == 0), stop=(k == 1))
                    ins.then_inc(S("mid_raw"), 1)
                if u >= LAG:
                    v = u - LAG
                    e, g = v // FG, v % FG
                    pe.wait_ge(S("mid"), v + 1)
                    for m in range(KC):
                        ins = mm(ps[:, 6 + m, 0:N], ring2[:, e % RING, g, m * P:(m + 1) * P],
                                 mid[:, v % MID, :], start=False, stop=(v == E * FG - 1), skip_group_check=True)
                        if v == E * FG - 1:
                            ins.then_inc(S("moe"), 1)
                        elif m == 1:
                            ins.then_inc(S("mid_used"), 1)
            for h in range(2):
                pe.wait_ge(S("moe_T"), 2)
                for i in (2 * h, 2 * h + 1):
                    for m in range(KC):
                        ins = nc.tensor.transpose(ps[0:R, h, (i % 2) * D + m * P:(i % 2) * D + (m + 1) * P],
                                                  yT[:, m, i * R:(i + 1) * R], ident)
                ins.then_inc(S("moe_turned"), 1)


def _turned(w):
    o, i = w.shape
    return np.ascontiguousarray(w.T.reshape(i // P, P, o).transpose(1, 0, 2))


def _halves(v):
    return v.reshape(-1, P).T


def _layout(x):
    f = {k: np.asarray(v) for k, v in x.items()}
    a = {}
    xp = np.zeros((B, WIN * (NG - 1) + P), np.float32)
    xp[:, K1 // 2:K1 // 2 + L] = f["x"][:, 0, :]
    a["xw"] = np.stack([xp[:, WIN * g:WIN * g + P].T for g in range(NG)], 1)
    w = np.zeros((P, NJ, TM, C1), np.float32)
    for j in range(NJ):
        for t in range(TM):
            s = (j * TM + t) * S1
            w[s:s + K1, j, t, :] = f["L0_tok_w1"][:, 0, :].T
    a["w1"] = w.reshape(P, NJ, P)
    w = np.zeros((TM, C1, 2, 2, C2), np.float32)
    for t in range(TM):
        for s in range(2):
            k = t + 4 * s - 1
            if k >= 0:
                w[t, :, s, :, :] = f["L0_tok_w2"][:, :, k].T[:, None, :]
    a["w2"] = w.reshape(P, 2, P)
    w = np.zeros((2, C2, 5, D), np.float32)
    for k in range(K3):
        w[k % 2, :, k // 2, :] = f["L0_tok_w3"][:, :, k].T
    a["w3"] = w.reshape(P, 5, D)
    w = np.zeros((P, KC, 3, P), np.float32)
    for g in range(D // 8):
        m, c = g // 16, (g % 16) * 8
        w[c:c + 8, m, :, c:c + 8] = f["L0_tok_w4"][g * 8:g * 8 + 8].transpose(1, 2, 0)
    a["w4"] = w
    a["w5"] = _turned(f["L0_tok_w5"][:, :, 0])
    by_head = np.arange(D).reshape(DA, HA).T.ravel()
    qkv = np.concatenate([f["L0_attn_w_qkv"][s * D + by_head] for s in range(3)], 0)
    bqkv = [f["L0_attn_b_qkv"][s * D + by_head] for s in range(3)]
    a["wqkv0"] = _turned(qkv)
    a["wo0"] = _turned(f["L0_attn_w_o"])
    a["f1"] = _turned(f["L0_ffn_w1"]).reshape(P, -1)
    a["f2"] = _turned(f["L0_ffn_w2"]).reshape(P, -1)
    a["wA"] = np.concatenate([_turned(f["L1_attn_W" + c]) for c in "qkvo"], 2)
    a["wB"] = np.concatenate([_turned(f["L1_ffn_w" + c].T) for c in "qkvo"], 2)
    a["gw"] = _turned(f["L1_ffn_gate_w"].T)
    a["e1"] = np.ascontiguousarray(f["L1_ffn_w1"].reshape(E, KC, P, FF).transpose(0, 2, 1, 3))
    a["e2"] = np.ascontiguousarray(f["L1_ffn_w2"].reshape(E, FG, P, D).transpose(0, 2, 1, 3))
    a["eb2"] = f["L1_ffn_b2"]
    c = {
        "b1": np.tile(f["L0_tok_b1"], TM)[:, None], "b2": np.tile(f["L0_tok_b2"], 2)[:, None],
        "b3": _halves(f["L0_tok_b3"]), "b4": _halves(f["L0_tok_b4"]),
        "bq0": _halves(bqkv[0]), "bk0": _halves(bqkv[1]),
        "cw": f["L0_ffn_conv_w"].reshape(FG, P, 3).transpose(1, 0, 2).reshape(P, 24),
        "cb": _halves(f["L0_ffn_conv_b"]),
        "bq1": _halves(f["L1_attn_bq"]), "bk1": _halves(f["L1_attn_bk"]),
        "g1": _halves(f["L1_ffn_ln1_g"]), "h1": _halves(f["L1_ffn_ln1_b"]),
        "bq2": _halves(f["L1_ffn_bq"]), "bk2": _halves(f["L1_ffn_bk"]),
        "g2": _halves(f["L1_ffn_ln2_g"]), "h2": _halves(f["L1_ffn_ln2_b"]),
        "eb1": _halves(f["L1_ffn_b1"]),
    }
    a["cols"] = np.concatenate([c[n] for n, _ in COLS], 1)
    r = {"b5": f["L0_tok_b5"], "nw": f["L0_tok_norm_w"], "bv0": bqkv[2], "bo0": f["L0_attn_b_o"],
         "bv1": f["L1_attn_bv"], "bo1": f["L1_attn_bo"], "bv2": f["L1_ffn_bv"], "bo2": f["L1_ffn_bo"],
         "gb": f["L1_ffn_gate_b"], "fr": f["L0_tok_rope_freqs"]}
    a["rows"] = np.concatenate([r[n] for n, _ in ROWS])
    p = np.arange(P)
    q = np.arange(R)
    con = {
        "ident": np.eye(P), "same": (p[:, None] // T == q[None] // T) * 1.0,
        "ohq": (p[:, None] % 32 == q[None] // T) * 1.0,
        "ohk": np.tile((p[:, None] % 32 != q[None] // T) * -BIG, (1, NT)),
        "par": np.stack([(p // DB % 2 == 0), (p // DB % 2 == 1)], 1) * 1.0,
        "tpos": (p % T)[:, None] * 1.0, "rank": np.tile(E - np.arange(E), (P, 1)) * 1.0,
    }
    a["con"] = np.concatenate([con[n] for n, _ in CONST], 1).astype(np.float32)
    return {k: np.ascontiguousarray(v) for k, v in a.items()}


def kernel(**inputs):
    import concourse.bacc as _bacc
    from concourse import mybir as _mybir
    from concourse.bass_utils import run_bass_kernel_spmd as _run

    nc = _bacc.Bacc("TRN2", target_bir_lowering=False, num_devices=1)
    arrays, aps = {}, {}
    for name, v in _layout(inputs).items():
        arrays[f"in_{name}"] = v
        aps[name] = nc.dram_tensor(f"in_{name}", v.shape, _mybir.dt.from_np(v.dtype), kind="ExternalInput").ap()
    out = nc.dram_tensor("out", (B, T, D), F32, kind="ExternalOutput").ap()
    tower(nc, aps, out)
    r = _run(nc, [arrays], core_ids=[0])
    return r.results[0]["out"]
```

```python
from contextlib import ExitStack

import numpy as np

import concourse.bass as bass
from concourse import mybir

F32 = mybir.dt.float32
BF16 = mybir.dt.bfloat16
F32R = mybir.dt.float32r
I32 = mybir.dt.int32
ALU = mybir.AluOpType
ACT = mybir.ActivationFunctionType
AX = mybir.AxisListType

P = 128
B, L = 64, 750
T = 5
D = 256
KC = D // P
NT = 4
BT = B // NT
R = BT * T
N = B * T
C1, K1, S1 = 32, 15, 8
C2, K2, S2 = 64, 7, 4
K3, S3 = 9, 5
TM = P // C1
NG, NJ = 8, 3
WIN = NJ * TM * S1
L1, L2 = 94, 24
HA = 8
HB = 16
DB = D // HB
FF = 1024
FG = FF // P
E = 8
CAP = 128
ROUNDS = -(-N // CAP)
RING = 3
AWAKE = 3
PRELOADS = 8
ROUND = 12582912.0
PI = float(np.pi)
TURN = [6.28125]
TURN.append(float((np.float32(2 * np.pi - TURN[0]).view(np.uint32) & np.uint32(0xFFFFF000)).view(np.float32)))
TURN.append(float(np.float32(2 * np.pi - TURN[0] - TURN[1])))

COLS = [("b1", 1), ("b2", 1), ("b3", 2), ("b4", 2), ("cw", 24), ("cb", 8),
        ("g1", 2), ("h1", 2), ("g2", 2), ("h2", 2),
        ("eb1", 64)]
ROWS = [("b5", D), ("nw", D), ("bo0", D), ("bo1", D), ("bo2", D),
        ("gb", E), ("fr", 8)]
CONST = [("ident", P), ("tpos", 1), ("rank", E), ("before", R), ("slot", E), ("slots", E * CAP)]


def places(table):
    at, out = 0, {}
    for name, n in table:
        out[name] = (at, n)
        at += n
    return out, at


COL, NCOL = places(COLS)
ROW, NROW = places(ROWS)
CON, NCON = places(CONST)


def tower(nc, a, out):
    with ExitStack() as ctx:
        def sb(name, shape, dt=F32):
            return ctx.enter_context(nc.sbuf_tensor(name, shape, dt))

        sems = {}

        def S(name):
            if name not in sems:
                sems[name] = ctx.enter_context(nc.semaphore(name))
            return sems[name]

        ps = ctx.enter_context(nc.psum_tensor("ps", [P, 8, 512], F32))

        xw = sb("xw", [P, NG, B])
        w1 = sb("w1", [P, NJ, P])
        w2 = sb("w2", [P, 2, P])
        w3 = sb("w3", [P, 5, D])
        w4 = sb("w4", [P, KC, 3, P])
        w5 = sb("w5", [P, KC, D])
        wqkv = [sb(f"wqkv{l}", [P, KC, 2, 3 * P]) for l in range(3)]
        wo = [sb(f"wo{l}", [P, KC, D]) for l in range(3)]
        bqkv = sb("bqkv", [P, 3, 3 * P])
        f1 = sb("f1", [P, KC * FF])
        f2 = sb("f2", [P, FG * D])
        fq = sb("fq", [P, 2 * KC * FF], BF16)
        f1q, f2q = fq[:, 0:KC * FF], fq[:, KC * FF:]
        gw = sb("gw", [P, KC, E])
        ring1 = sb("ring1", [P, RING, KC, FF])
        ring2 = sb("ring2", [P, RING, FG, D])
        eb2 = sb("eb2", [E, D])
        cols = sb("cols", [P, NCOL])
        rows = sb("rows", [R, NROW])
        con = sb("con", [P, NCON])
        identb = sb("identb", [P, P], BF16)
        ones = sb("ones", [P, P])
        onesb = sb("onesb", [P, P], BF16)

        def col(name, i=0, p=slice(None)):
            at = COL[name][0] + i
            return cols[p, at:at + 1]

        def row(name):
            at, n = ROW[name]
            return rows[:, at:at + n]

        def cst(name, p=slice(None)):
            at, n = CON[name]
            return con[p, at:at + n]

        ident = cst("ident")

        ARENA = max(78 * B, 2 * FG * N)
        arena = sb("arena", [P, ARENA])
        H1 = arena[:, 0:25 * B].rearrange("p (u b) -> p u b", b=B)
        H2 = arena[:, 25 * B:54 * B].rearrange("p (u b) -> p u b", b=B)
        H3 = arena[:, 54 * B:68 * B].rearrange("p (m u b) -> p m u b", m=KC, b=B)
        H4 = arena[:, 68 * B:78 * B].rearrange("p (m n) -> p m n", m=KC)
        prod = arena[:, 0:T * T * P].rearrange("p (i j f) -> p i j f", i=T, j=T)
        ropet = arena[0:R, NT * D:2 * NT * D].rearrange("p (u c h k) -> p u c h k", u=2, c=2, k=8)
        junk = arena[0:R, 0:NT * D].rearrange("p (i d) -> p i d", i=NT)
        hid = arena[:, 0:FG * N].rearrange("p (g n) -> p g n", g=FG)
        hidc = arena[:, FG * N:2 * FG * N].rearrange("p (g n) -> p g n", g=FG)

        X = sb("X", [R, NT, D])
        Y = sb("Y", [R, NT, D])
        Z = sb("Z", [R, NT, D])
        Zq = sb("Zq", [R, NT, D], BF16)
        ZT = sb("ZT", [P, KC, N])
        ZqT = sb("ZqT", [P, KC, N], BF16)
        QKV = sb("QKV", [P, T, 3, P])
        SC = sb("SC", [P, T, T, 8])
        smax = sb("smax", [P, T, 8])
        OT = sb("OT", [P, KC, N])
        hq = sb("hq", [P, FG, N], BF16)
        mx1 = sb("mx1", [P, N])
        bc = sb("bc", [P, N])
        diag = sb("diag", [R, NT, R])
        st = sb("st", [R, NT, 6])
        mv = sb("mv", [R, NT, 2])
        ve = sb("ve", [R, 2, NT])
        warm = sb("warm", [1, PRELOADS])
        sd = sb("sd", [R, 2, NT])
        rs = sb("rs", [R, 2, NT])
        rt = sb("rt", [R, 2, NT])
        amax = sb("amax", [R, NT])
        qs = sb("qs", [R, NT])
        iv = sb("iv", [R, NT])
        ang = sb("ang", [R, 2, 8])
        trn = sb("trn", [R, 2, 8])
        cs = sb("cs", [R, 2, 8])
        wsum = sb("wsum", [P, 2])
        wsc = sb("wsc", [P, 2])
        wiv = sb("wiv", [P, 2])
        cwq = sb("cwq", [P, 24])
        lg = sb("lg", [R, NT, E])
        lm = sb("lm", [R, NT])
        oh = sb("oh", [R, NT, E])
        ohT = sb("ohT", [E, N])
        ohb = sb("ohb", [R, NT, E], BF16)
        beforeb = sb("beforeb", [R, R], BF16)
        place = sb("place", [R, NT])
        first = sb("first", [R, NT])
        key = sb("key", [R, NT])
        kin = sb("kin", [R, NT])
        most = sb("most", [R, 1])
        mosti = sb("mosti", [R, 1], I32)
        keyb = sb("keyb", [P, N])
        zhi = sb("zhi", [R, NT, D], F32R)
        zlo = sb("zlo", [R, NT, D], F32R)
        perm = sb("perm", [R, 2, NT, CAP], F32R)
        permT = sb("permT", [P, 2, N], F32R)
        yhi = sb("yhi", [P, 2, D], F32R)
        ylo = sb("ylo", [P, 2, D], F32R)
        xe = arena[:, 2 * FF:2 * FF + 2 * D].rearrange("p (s k n) -> p s k n", s=2, k=KC)
        mid = arena[:, 0:2 * FF].rearrange("p (s g n) -> p s g n", s=2, g=FG)
        FFB = [3, 4, 5, 6, 7, 3, 4, 5]
        block = ctx.enter_context(nc.Block())

        def rounds(eng, work):
            work(0)
            eng.wait_ge(S("most"), 1)
            most_of_one = eng.value_load(mosti[0:1, 0:1], min_val=0, max_val=N)
            for r in range(1, ROUNDS):
                with eng.If(most_of_one > r * CAP):
                    work(r)

        @block.sync
        def _(sp):
            def load(dst, name, sem):
                sp.dma_start(dst, a[name]).then_inc(S(sem), 16)

            load(xw[:], "xw", "ld_x")
            load(w1[:], "w1", "ld_x")
            load(cols[:], "cols", "ld_cols")
            load(w2[:], "w2", "ld_w2")
            load(w3[:], "w3", "ld_w3")
            load(w4[:], "w4", "ld_w4")
            load(con[:], "con", "ld_con")
            load(w5[:], "w5", "ld_w5")
            sp.dma_start(rows[:], a["rows"].partition_broadcast(R)).then_inc(S("ld_rows"), 16)
            load(f1[:], "f1", "ld_f1")
            for h in range(2):
                sp.dma_start(bqkv[64 * h:64 * h + 64], a["bqkv"][h].partition_broadcast(64)).then_inc(S("ld_bqkv"), 16)
            load(f2[:], "f2", "ld_f2")
            load(wqkv[0][:], "wqkv0", "ld_a0")
            load(wo[0][:], "wo0", "ld_a0")
            for l in (1, 2):
                load(wqkv[l][:], f"wqkv{l}", f"ld_a{l}")
                load(wo[l][:], f"wo{l}", f"ld_a{l}")
            load(gw[:], "gw", "ld_gw")
            load(eb2[:], "eb2", "ld_gw")

            def experts(r):
                for x in range(r * E, (r + 1) * E):
                    if x >= RING:
                        sp.wait_ge(S("down"), x - RING + 1)
                    sp.dma_start(ring1[:, x % RING], a["e1"][x % E]).then_inc(S(f"ld_e{x % RING}"), 16)
                    sp.dma_start(ring2[:, x % RING], a["e2"][x % E]).then_inc(S(f"ld_e{x % RING}"), 16)

            rounds(sp, experts)
            o = out.rearrange("(i b) t d -> (b t) i d", i=NT)
            for i in range(NT):
                sp.wait_ge(S("out_ready"), i + 1)
                sp.dma_start(o[:, i, :], Y[:, i, :]).then_inc(S("stored"), 16)
            sp.wait_ge(S("stored"), 16 * NT)

        @block.gpsimd
        def _(pool):
            n = [0]

            def step(ins):
                n[0] += 1
                ins.then_inc(S("pool_steps"), 1)

            def settle():
                pool.wait_ge(S("pool_steps"), n[0])

            for dst, done in ((H1[:, 0, :], None), (H1[64:128, 24, :], "h1_zeros"), (H2[0:64, 0:4, :], None),
                              (H2[0:64, 28, :], None), (H2[64:128, 0:3, :], None),
                              (H2[64:128, 27:29, :], None), (H3[:, :, 0, :], None), (H3[:, :, 6, :], "h3_zeros")):
                step(nc.gpsimd.memset(dst, 0.0))
                settle()
                if done:
                    pool.sem_inc(S(done), 1)
            step(nc.gpsimd.memset(ones[:], 1.0))
            step(nc.gpsimd.memset(onesb[:], 1.0))
            settle()
            pool.sem_inc(S("ones"), 1)
            for w, (src, dst) in enumerate(((f1, f1q), (f2, f2q))):
                pool.wait_ge(S("w_scale"), w + 1)
                step(nc.gpsimd.tensor_scalar(src[:], src[:], wsc[:, w:w + 1], ROUND, ALU.mult, ALU.add))
                settle()
                step(nc.gpsimd.tensor_scalar(src[:], src[:], ROUND, 1.0, ALU.subtract, ALU.min))
                settle()
                nc.gpsimd.tensor_scalar(dst[:], src[:], -1.0, None, ALU.max).then_inc(S("w_ternary"), 1)

            def add_bias(name, done, before):
                pool.wait_ge(S(done), before)
                nc.gpsimd.tensor_tensor(X[:], X[:], row(name).unsqueeze(1).to_broadcast([R, NT, D]),
                                        ALU.add).then_inc(S("residual"), 1)

            add_bias("bo0", "ln0_z", NT)
            add_bias("bo1", "ln2_z", NT)
            pool.wait_ge(S("ln3_z"), NT)
            step(nc.gpsimd.tensor_copy(Y[:], X[:]))
            settle()
            for i in range(NT):
                ins = nc.gpsimd.tensor_scalar(X[:, i, :], X[:, i, :], mv[:, i, 0:1], rs[:, 1, i:i + 1],
                                              ALU.subtract, ALU.mult)
            step(ins)
            add_bias("bo2", "pool_steps", n[0])
            pool.wait_ge(S("attended2"), 1)
            nc.gpsimd.tensor_tensor(Y[:], Y[:], X[:], ALU.add).then_inc(S("residual"), 1)

        @block.scalar
        def _(act):
            def copy_out(dst, src):
                return nc.scalar.activation(dst, src, ACT.Identity)

            loads = [0]

            def preload(func):
                nc.scalar.activation(warm[:, loads[0]:loads[0] + 1], con[0:1, 0:1], func)
                loads[0] += 1

            act.wait_ge(S("ld_cols"), 16)
            act.wait_ge(S("h1_zeros"), 1)
            for j in range(NJ):
                act.wait_ge(S("conv1"), j + 1)
                src = ps[:, j, :].rearrange("p (g b) -> p g b", b=B)
                if j < NJ - 1:
                    nc.scalar.activation(H1[:, 1 + j:23 + j:3, :], src, ACT.Gelu,
                                         bias=col("b1")).then_inc(S("h1"), 1)
                else:
                    nc.scalar.activation(H1[:, 3:22:3, :], src[:, 0:7, :], ACT.Gelu, bias=col("b1"))
                    nc.scalar.activation(H1[0:64, 24, :], src[0:64, 7, :], ACT.Gelu,
                                         bias=col("b1", 0, slice(0, 64))).then_inc(S("h1"), 1)
            act.wait_ge(S("h3_zeros"), 1)
            for q in range(3):
                act.wait_ge(S("conv2"), q + 1)
                src = ps[:, 3 + q, :].rearrange("p (u b) -> p u b", b=B)
                nc.scalar.activation(H2[0:64, 4 + 8 * q:12 + 8 * q, :], src[0:64], ACT.Gelu,
                                     bias=col("b2", 0, slice(0, 64)))
                nc.scalar.activation(H2[64:128, 3 + 8 * q:11 + 8 * q, :], src[64:128], ACT.Gelu,
                                     bias=col("b2", 0, slice(64, 128))).then_inc(S("h2"), 1)
            for m in range(KC):
                act.wait_ge(S("conv3"), m + 1)
                nc.scalar.activation(H3[:, m, 1:6, :], ps[:, 6 + m, 0:N].rearrange("p (t b) -> p t b", b=B),
                                     ACT.Gelu, bias=col("b3", m)).then_inc(S("h3"), 1)
            for m in range(KC):
                act.wait_ge(S("conv4"), m + 1)
                nc.scalar.activation(H4[:, m, :].rearrange("p (b t) -> p t b", t=T),
                                     ps[:, m, 0:N].rearrange("p (t b) -> p t b", b=B),
                                     ACT.Gelu, bias=col("b4", m)).then_inc(S("h4"), 1)
            act.wait_ge(S("ld_con"), 16)
            act.wait_ge(S("angles"), 1)
            nc.scalar.activation(cs[:], ang[:], ACT.Sin).then_inc(S("sincos"), 1)
            preload(ACT.Gelu)
            for h in range(2):
                act.wait_ge(S("conv5_biased"), h + 1)
                nc.scalar.activation(Y[:, 2 * h:2 * h + 2, :], Y[:, 2 * h:2 * h + 2, :],
                                     ACT.Gelu).then_inc(S("h5"), 1)
            preload(ACT.Sqrt)
            for i in range(NT):
                act.wait_ge(S("roped"), i // 2 + 1)
                ins = nc.scalar.activation(junk[:, i], Z[:, i, :], ACT.Square, accum_out=ve[:, 0, i:i + 1])
            ins.then_inc(S("squares"), 1)

            def root(tag, m=1):
                act.wait_ge(S(tag + "_var"), 1)
                nc.scalar.activation(sd[:, 0:m], ve[:, 0:m], ACT.Sqrt, scale=4.0).then_inc(S(tag + "_root"), 1)

            def half_T(tag, affine=None):
                act.wait_ge(S(tag + "_turned"), 1)
                if affine:
                    nc.scalar.activation(ZT[:, 0, :], ps[:, 0, 0:N], ACT.Identity, bias=col(affine[1], 0),
                                         scale=col(affine[0], 0)).then_inc(S(tag + "_T"), 1)
                else:
                    copy_out(ZT[:, 0, :], ps[:, 0, 0:N]).then_inc(S(tag + "_T"), 1)

            root("rms")
            root("ln0")
            half_T("ln0")

            def attended(l):
                act.wait_ge(S("mixed"), 2 * l + 1)
                copy_out(OT[:].rearrange("p h (b t) -> p t h b", t=T)[:, 0:4],
                         ps[:, 5, :].rearrange("p (t h b) -> p t h b", t=4, h=2)).then_inc(S("mixed_T"), 1)

            attended(0)

            root("ln1")
            preload(ACT.Silu)
            act.wait_ge(S("zq_turned"), 1)
            copy_out(ZqT[:, 0, :], ps[:, 0, :].bitcast(BF16)[:, 0:N]).then_inc(S("zq_T"), 1)
            for g in range(FG):
                act.wait_ge(S("hid_scaled"), g + 1)
                nc.scalar.activation(hidc[:, g, :], hid[:, g, :], ACT.Identity, bias=col("cb", g),
                                     scale=cwq[:, 3 * g + 1:3 * g + 2]).then_inc(S("tap1"), 1)
            for g in range(FG):
                act.wait_ge(S("conv_done"), g + 1)
                nc.scalar.activation(hid[:, g, :], hidc[:, g, :], ACT.Silu).then_inc(S("silu"), 1)

            preload(ACT.Sqrt)

            def softmax_attention(l):
                preload(ACT.Exp)
                act.wait_ge(S("less"), l)
                nc.scalar.activation(SC[:], SC[:], ACT.Exp, scale=DB ** -0.5).then_inc(S("exp"), 1)
                preload(ACT.Sqrt)
                attended(l)

            root("ln2")
            half_T("ln2")
            softmax_attention(1)
            root("ln3", 2)
            half_T("ln3", ("g1", "h1"))
            softmax_attention(2)
            root("ln4")
            half_T("ln4", ("g2", "h2"))

            act.wait_ge(S("oh_turned"), 1)
            copy_out(ohT[:], ps[0:E, 3, 0:N]).then_inc(S("oh_T"), 1)

            def experts(r):
                def gathered(x):
                    act.wait_ge(S("gathered"), x + 1)
                    if x >= 2:
                        act.wait_ge(S("up"), 2 * (x - 1))
                    for k in range(KC):
                        ins = nc.scalar.activation(xe[:, x % 2, k, :], ps[:, x % 2, k * CAP:(k + 1) * CAP],
                                                   ACT.Identity, bias=col("h2", k), scale=col("g2", k))
                    ins.then_inc(S("xe"), 1)

                gathered(r * E)
                for x in range(r * E, (r + 1) * E):
                    act.wait_ge(S("up"), 2 * x + 1)
                    if x >= 2:
                        act.wait_ge(S("down"), x - 1)
                    for g in range(4):
                        ins = nc.scalar.activation(mid[:, x % 2, g, :], ps[:, 2, g * CAP:(g + 1) * CAP], ACT.Relu,
                                                   bias=col("eb1", x % E * FG + g))
                    ins.then_inc(S("mid_a"), 1)
                    if x + 1 < (r + 1) * E:
                        gathered(x + 1)

            rounds(act, experts)

        @block.vector
        def _(dve):
            n = [0]

            def step(ins):
                n[0] += 1
                ins.then_inc(S("dve_steps"), 1)

            def settle(but=0):
                dve.wait_ge(S("dve_steps"), n[0] - but)

            V_ = nc.vector
            dve.wait_ge(S("ld_con"), 16)
            V_.tensor_copy(beforeb[:], cst("before", slice(0, R)))
            V_.tensor_copy(identb[:], ident).then_inc(S("const_bf"), 1)
            dve.wait_ge(S("ld_rows"), 16)
            for s in range(2):
                step(V_.tensor_scalar(ang[:, s, :], row("fr"), cst("tpos", slice(0, R)), None, ALU.mult))
            settle()
            step(V_.tensor_scalar(trn[:, 0, :], ang[:, 0, :], 1.0 / (2 * PI), 0.25, ALU.mult, ALU.add))
            step(V_.tensor_scalar(trn[:, 1, :], ang[:, 1, :], 1.0 / (2 * PI), None, ALU.mult))
            settle()
            step(V_.tensor_scalar(trn[:], trn[:], ROUND, None, ALU.add))
            settle()
            step(V_.tensor_scalar(trn[:], trn[:], ROUND, None, ALU.subtract))
            settle()
            for c in TURN:
                step(V_.scalar_tensor_tensor(out=ang[:], in0=trn[:], scalar=-c, in1=ang[:],
                                             op0=ALU.mult, op1=ALU.add))
                settle()
            step(V_.tensor_scalar(ang[:, 0, :], ang[:, 0, :], PI / 2, None, ALU.add))
            settle()
            V_.tensor_scalar(ang[:], ang[:], 3.1415925, -3.1415925, ALU.min, ALU.max).then_inc(S("angles"), 1)

            dve.wait_ge(S("ld_f1"), 16)
            V_.tensor_reduce(wsum[:, 0:1], f1[:], AX.X, ALU.add, apply_absolute_value=True)
            dve.wait_ge(S("ld_f2"), 16)
            V_.tensor_reduce(wsum[:, 1:2], f2[:], AX.X, ALU.add, apply_absolute_value=True).then_inc(S("w_sums"), 1)

            dve.wait_ge(S("w_total"), 1)
            step(V_.tensor_scalar(wiv[:], ps[:, 4, 0:2], 1.0 / (FF * D), 1e-5, ALU.mult, ALU.max))
            settle()
            step(V_.reciprocal(wsc[:], wiv[:]))
            settle()
            V_.tensor_scalar(cwq[:], cols[:, COL["cw"][0]:COL["cw"][0] + 24], wiv[:, 0:1], None,
                             ALU.mult).then_inc(S("w_scale"), 2)

            b5 = row("b5").unsqueeze(1).to_broadcast([R, 2, D])

            def b5_add(h):
                dve.wait_ge(S("conv5"), h + 1)
                V_.tensor_tensor(Y[:, 2 * h:2 * h + 2, :], ps[0:R, 2 + h, :].rearrange("p (i d) -> p i d", i=2),
                                 b5, ALU.add).then_inc(S("conv5_biased"), 1)

            dve.wait_ge(S("sincos"), 1)
            cosb = cs[:, 0, :].unsqueeze(1).to_broadcast([R, 2 * HB, 8])
            sinb = cs[:, 1, :].unsqueeze(1).to_broadcast([R, 2 * HB, 8])
            for h in range(2):
                b5_add(h)
                dve.wait_ge(S("h5"), h + 1)
                yv = Y[:, 2 * h:2 * h + 2].rearrange("p i (h k c) -> p (i h) k c", h=HB, c=2)
                zv = Z[:, 2 * h:2 * h + 2].rearrange("p i (h k c) -> p (i h) k c", h=HB, c=2)
                t0, t1 = ropet[:, h, 0], ropet[:, h, 1]
                step(V_.tensor_tensor(t0, yv[:, :, :, 1], sinb, ALU.mult))
                step(V_.tensor_tensor(t1, yv[:, :, :, 1], cosb, ALU.mult))
                step(V_.tensor_tensor(zv[:, :, :, 0], yv[:, :, :, 0], cosb, ALU.mult))
                step(V_.tensor_tensor(zv[:, :, :, 1], yv[:, :, :, 0], sinb, ALU.mult))
                settle()
                step(V_.tensor_tensor(zv[:, :, :, 0], zv[:, :, :, 0], t0, ALU.subtract))
                V_.tensor_tensor(zv[:, :, :, 1], zv[:, :, :, 1], t1, ALU.add).then_inc(S("roped"), 1)

            def inverse_root(tag, m=1):
                r_, t_, v_, s_ = rs[:, 0:m], rt[:, 0:m], ve[:, 0:m], sd[:, 0:m]
                dve.wait_ge(S(tag + "_root"), 1)
                step(V_.reciprocal(rt[:, 0:m], sd[:, 0:m]))
                settle()
                step(V_.tensor_tensor(t_, t_, v_, ALU.mult))
                settle()
                step(V_.scalar_tensor_tensor(out=t_, in0=s_, scalar=0.25, in1=t_, op0=ALU.mult, op1=ALU.add))
                settle()
                step(V_.reciprocal(r_, t_))
                settle()

            dve.wait_ge(S("squares"), 1)
            V_.tensor_scalar(ve[:, 0], ve[:, 0], 1.0 / D, 1e-8, ALU.mult, ALU.add).then_inc(S("rms_var"), 1)
            inverse_root("rms")
            for i in range(NT):
                step(V_.scalar_tensor_tensor(out=X[:, i, :], in0=Z[:, i, :], scalar=rs[:, 0, i:i + 1],
                                             in1=row("nw"), op0=ALU.mult, op1=ALU.mult))
            settle()

            def stats(tiles):
                for i in tiles:
                    step(V_.bn_stats(st[:, i, :], X[:, i, :]))

            def layernorm(tag, twice=False):
                settle()
                for i in range(NT):
                    step(V_.bn_aggr(mv[:, i, :], st[:, i, :]))
                settle()
                if twice:
                    step(V_.tensor_scalar(ve[:, 1], mv[:, :, 1], 1e-5, None, ALU.add))
                    settle()
                    V_.scalar_tensor_tensor(out=ve[:, 0], in0=ve[:, 1], scalar=1e-5, in1=mv[:, :, 1],
                                            op0=ALU.mult, op1=ALU.add).then_inc(S(tag + "_var"), 1)
                else:
                    V_.tensor_scalar(ve[:, 0], mv[:, :, 1], 1e-5, None, ALU.add).then_inc(S(tag + "_var"), 1)
                dve.wait_ge(S(tag + "_var"), 1)
                inverse_root(tag, 1 + twice)
                for i in range(NT):
                    V_.tensor_scalar(Z[:, i, :], X[:, i, :], mv[:, i, 0:1], rs[:, 0, i:i + 1],
                                     ALU.subtract, ALU.mult).then_inc(S(tag + "_z"), 1)

            def half_T(tag, affine=None):
                dve.wait_ge(S(tag + "_turned"), 2)
                if affine:
                    V_.tensor_scalar(ZT[:, 1, :], ps[:, 1, 0:N], col(affine[0], 1), col(affine[1], 1),
                                     ALU.mult, ALU.add).then_inc(S(tag + "_T"), 1)
                else:
                    V_.tensor_copy(ZT[:, 1, :], ps[:, 1, 0:N]).then_inc(S(tag + "_T"), 1)

            def add_out(sem, before, banks):
                dve.wait_ge(S("residual"), before // 2 + 1)
                for h in range(2):
                    dve.wait_ge(S(sem), before + h + 1)
                    step(V_.tensor_tensor(X[:, 2 * h:2 * h + 2, :],
                                          ps[0:R, banks + h, :].rearrange("p (i d) -> p i d", i=2),
                                          X[:, 2 * h:2 * h + 2, :], ALU.add))
                    settle()
                    stats((2 * h, 2 * h + 1))

            stats(range(NT))
            layernorm("ln0")
            half_T("ln0")

            def attention(l, heads, bank_out):
                hh = heads // 2
                dh = D // heads
                sc = SC[:, :, :, 0:hh] if hh < 8 else SC[:]

                def sums(i, j):
                    step(V_.tensor_reduce(sc[:, i, j], prod[:, i, j].rearrange("p i j (h d) -> p i j h d", d=dh),
                                          AX.X, ALU.add))

                for t in range(T):
                    now, past, upto = slice(t, t + 1), slice(0, t), slice(0, t + 1)
                    dve.wait_ge(S("qkv"), T * l + t + 1)
                    step(V_.tensor_tensor(QKV[:, t].rearrange("p c f -> p (c f)"), ps[:, t, 0:3 * P], bqkv[:, l, :],
                                          ALU.add))
                    if t:
                        settle(1)
                        sums(slice(t - 1, t), past)
                        if t > 1:
                            sums(slice(0, t - 1), slice(t - 1, t))
                    settle(min(t, 2))
                    step(V_.tensor_tensor(prod[:, t, upto], QKV[:, t, 0:1, :].to_broadcast([P, t + 1, P]),
                                          QKV[:, upto, 1, :], ALU.mult))
                    if t:
                        step(V_.tensor_tensor(prod[:, past, t], QKV[:, past, 0, :],
                                              QKV[:, now, 1, :].to_broadcast([P, t, P]), ALU.mult))
                settle()
                dve.sem_inc(S("attending"), 1)
                sums(slice(T - 1, T), slice(0, T))
                sums(slice(0, T - 1), slice(T - 1, T))
                settle()
                dve.sem_inc(S("attending"), 1)
                scv = sc
                if l:
                    step(V_.tensor_reduce(smax[:], scv.rearrange("p i j h -> p i h j"), AX.X, ALU.max))
                    settle()
                    V_.tensor_tensor(scv, scv, smax[:].unsqueeze(2).to_broadcast([P, T, T, hh]),
                                     ALU.subtract).then_inc(S("less"), 1)
                    dve.wait_ge(S("exp"), l)
                    step(V_.tensor_reduce(smax[:], scv.rearrange("p i j h -> p i h j"), AX.X, ALU.add))
                    settle()
                    step(V_.reciprocal(smax[:], smax[:]))
                    settle()
                    step(V_.tensor_tensor(scv, scv, smax[:].unsqueeze(2).to_broadcast([P, T, T, hh]), ALU.mult))
                    settle()
                dve.sem_inc(S("attending"), 1)
                for i in range(T):
                    V_.tensor_tensor(prod[:, i].rearrange("p j (h d) -> p j h d", h=hh),
                                     QKV[:, :, 2, :].rearrange("p j (h d) -> p j h d", h=hh),
                                     scv[:, i].unsqueeze(3).to_broadcast([P, T, hh, dh]),
                                     ALU.mult).then_inc(S("weighted"), 1)
                dve.wait_ge(S("mixed"), 2 * l + 2)
                V_.tensor_copy(OT[:].rearrange("p h (b t) -> p h b t", t=T)[:, :, :, 4],
                               ps[:, 6, 0:P].rearrange("p (h b) -> p h b", h=2)).then_inc(S("mixed_T"), 1)
                add_out("projected", 2 * l, bank_out)

            dve.wait_ge(S("ld_bqkv"), 32)
            attention(0, HA, 0)

            def act_scale(tag):
                step(V_.tensor_scalar(amax[:], amax[:], 1e-5, None, ALU.max))
                settle()
                step(V_.reciprocal(qs[:], amax[:]))
                step(V_.tensor_scalar(iv[:], amax[:], 1.0 / 127.0, None, ALU.mult))
                settle()
                V_.tensor_scalar(qs[:], qs[:], 127.0, None, ALU.mult).then_inc(S(tag + "_scale"), 1)
                dve.wait_ge(S(tag + "_scale"), 1)

            def diagonal(sc, tag):
                V_.tensor_tensor(diag[:], ident[0:R, 0:R].unsqueeze(1).to_broadcast([R, NT, R]),
                                 sc[:].unsqueeze(2).to_broadcast([R, NT, R]), ALU.mult).then_inc(S(tag), 1)

            layernorm("ln1")
            dve.wait_ge(S("ln1_z"), NT)
            step(V_.tensor_reduce(amax[:], Z[:], AX.X, ALU.max, apply_absolute_value=True))
            settle()
            act_scale("zq")
            for i in range(NT):
                step(V_.tensor_scalar(Z[:, i, :], Z[:, i, :], qs[:, i:i + 1], ROUND, ALU.mult, ALU.add))
            settle()
            step(V_.tensor_scalar(Z[:], Z[:], ROUND, 127.0, ALU.subtract, ALU.min))
            settle()
            V_.tensor_scalar(Zq[:], Z[:], -128.0, None, ALU.max).then_inc(S("zq"), 1)
            diagonal(iv, "iv1_diag")
            dve.wait_ge(S("zq_turned"), 2)
            V_.tensor_copy(ZqT[:, 1, :], ps[:, 1, :].bitcast(BF16)[:, 0:N]).then_inc(S("zq_T"), 1)
            dve.wait_ge(S("iv1_bc"), 1)
            step(V_.tensor_copy(bc[:], ps[:, 2, 0:N]))
            settle()
            def taps(g):
                return (hid[:, g, :].rearrange("p (b t) -> p b t", t=T),
                        hidc[:, g, :].rearrange("p (b t) -> p b t", t=T))

            for g in range(FG + 2):
                if g < FG:
                    dve.wait_ge(S("ff1"), g + 1)
                    V_.tensor_tensor(hid[:, g, :], ps[:, FFB[g], 0:N], bc[:], ALU.mult).then_inc(S("hid_scaled"), 1)
                if 1 <= g <= FG:
                    src, dst = taps(g - 1)
                    dve.wait_ge(S("tap1"), g)
                    V_.scalar_tensor_tensor(out=dst[:, :, 1:T], in0=src[:, :, 0:T - 1],
                                            scalar=cwq[:, 3 * g - 3:3 * g - 2], in1=dst[:, :, 1:T],
                                            op0=ALU.mult, op1=ALU.add).then_inc(S("tap0"), 1)
                if g >= 2:
                    src, dst = taps(g - 2)
                    dve.wait_ge(S("tap0"), g - 1)
                    V_.scalar_tensor_tensor(out=dst[:, :, 0:T - 1], in0=src[:, :, 1:T],
                                            scalar=cwq[:, 3 * g - 4:3 * g - 3], in1=dst[:, :, 0:T - 1],
                                            op0=ALU.mult, op1=ALU.add).then_inc(S("conv_done"), 1)
            for h in range(2):
                dve.wait_ge(S("silu"), FG // 2 * (h + 1))
                step(V_.tensor_reduce(bc[:] if h else mx1[:],
                                      hid[:, FG // 2 * h:FG // 2 * (h + 1)].rearrange("p g n -> p n g"), AX.X,
                                      ALU.max, apply_absolute_value=True))
            settle()
            V_.tensor_tensor(mx1[:], mx1[:], bc[:], ALU.max).then_inc(S("mx1"), 1)
            dve.wait_ge(S("mx1_turned"), 1)
            step(V_.tensor_reduce(amax[:], ps[0:R, 0, :].rearrange("p (i c) -> p i c", i=NT), AX.X, ALU.max))
            settle()
            act_scale("hq")
            diagonal(qs, "qs2_diag")
            step(V_.tensor_scalar(iv[:], iv[:], wiv[0:R, 1:2], None, ALU.mult))
            dve.wait_ge(S("qs2_bc"), 1)
            step(V_.tensor_copy(bc[:], ps[:, 1, 0:N]))
            settle()
            for g in range(FG + 2):
                if g < FG:
                    step(V_.tensor_tensor(hid[:, g, :], hid[:, g, :], bc[:], ALU.mult))
                if 1 <= g <= FG:
                    settle(1)
                    step(V_.tensor_scalar(hid[:, g - 1, :], hid[:, g - 1, :], 127.0, -128.0, ALU.min, ALU.max))
                if g >= 2:
                    settle(min(2, FG + 1 - g))
                    V_.tensor_scalar(hq[:, g - 2, :], hid[:, g - 2, :], ROUND, ROUND,
                                     ALU.add, ALU.subtract).then_inc(S("hq"), 1)
            for i in range(NT):
                dve.wait_ge(S("ff2"), i // 2 + 1)
                step(V_.scalar_tensor_tensor(out=X[:, i, :], in0=ps[0:R, 2 + i // 2, (i % 2) * D:(i % 2 + 1) * D],
                                             scalar=iv[:, i:i + 1], in1=X[:, i, :],
                                             op0=ALU.mult, op1=ALU.add))
                if i % 2:
                    settle()
                    stats((i - 1, i))

            layernorm("ln2")
            half_T("ln2")
            attention(1, HB, 0)
            layernorm("ln3", twice=True)
            half_T("ln3", ("g1", "h1"))
            attention(2, HB, 0)
            dve.sem_inc(S("attended2"), 1)
            layernorm("ln4")
            half_T("ln4", ("g2", "h2"))

            dve.wait_ge(S("logits"), 1)
            step(V_.tensor_tensor(lg[:], ps[0:R, 2, 0:NT * E].rearrange("p (i e) -> p i e", i=NT),
                                  row("gb").unsqueeze(1).to_broadcast([R, NT, E]), ALU.add))
            settle()
            step(V_.tensor_reduce(lm[:], lg[:], AX.X, ALU.max))
            settle()
            step(V_.tensor_tensor(lg[:], lg[:], lm[:].unsqueeze(2).to_broadcast([R, NT, E]), ALU.is_equal))
            settle()
            step(V_.tensor_tensor(lg[:], lg[:], cst("rank", slice(0, R)).unsqueeze(1).to_broadcast([R, NT, E]),
                                  ALU.mult))
            settle()
            step(V_.tensor_reduce(lm[:], lg[:], AX.X, ALU.max))
            settle()
            step(V_.tensor_tensor(ohb[:], lg[:], lm[:].unsqueeze(2).to_broadcast([R, NT, E]), ALU.is_equal))
            V_.tensor_tensor(oh[:], lg[:], lm[:].unsqueeze(2).to_broadcast([R, NT, E]),
                             ALU.is_equal).then_inc(S("onehot"), 1)
            step(V_.tensor_scalar(first[:], lm[:], -float(CAP), float(CAP * E), ALU.mult, ALU.add))
            step(V_.tensor_copy(zhi[:], Z[:]))
            settle()
            V_.tensor_tensor(zlo[:], Z[:], zhi[:].bitcast(F32), ALU.subtract).then_inc(S("z_parts"), 1)
            dve.wait_ge(S("ranks"), 1)
            step(V_.tensor_reduce(most[:], ps[0:R, 4, NT * E:(NT + 1) * E], AX.X, ALU.max))
            step(V_.tensor_tensor(lg[:], ps[0:R, 4, 0:NT * E].rearrange("p (i e) -> p i e", i=NT), oh[:], ALU.mult))
            settle()
            V_.tensor_copy(mosti[:], most[:]).then_inc(S("most"), 1)
            step(V_.tensor_reduce(place[:], lg[:], AX.X, ALU.add))
            settle()

            def experts(r):
                step(V_.tensor_scalar(key[:], place[:], -float(CAP * r), None, ALU.add))
                settle()
                step(V_.tensor_scalar(kin[:], key[:], 0.0, None, ALU.is_ge))
                step(V_.scalar_tensor_tensor(out=lm[:], in0=key[:], scalar=1.0, in1=first[:],
                                             op0=ALU.add, op1=ALU.add))
                settle()
                step(V_.scalar_tensor_tensor(out=kin[:], in0=key[:], scalar=float(CAP), in1=kin[:],
                                             op0=ALU.is_lt, op1=ALU.mult))
                settle()
                step(V_.tensor_tensor(key[:], kin[:], lm[:], ALU.mult))
                settle()
                step(V_.tensor_scalar(key[:], key[:], 1.0, None, ALU.subtract))
                settle()
                V_.tensor_tensor(diag[:], ident[0:R, 0:R].unsqueeze(1).to_broadcast([R, NT, R]),
                                 key[:].unsqueeze(2).to_broadcast([R, NT, R]), ALU.mult).then_inc(S("key_diag"), 1)

                def chooser(x):
                    if x >= 2:
                        dve.wait_ge(S("gathered"), x - 1)
                    at = CON["slots"][0] + x % E * CAP
                    V_.tensor_tensor(perm[:, x % 2], con[0:R, at:at + CAP].unsqueeze(1).to_broadcast([R, NT, CAP]),
                                     key[:].unsqueeze(2).to_broadcast([R, NT, CAP]),
                                     ALU.is_equal).then_inc(S("perm"), 1)

                def chooser_T(x):
                    if x >= 2:
                        dve.wait_ge(S("scattered"), x - 1)
                    at = CON["slot"][0] + x % E
                    V_.tensor_scalar(permT[:, x % 2, :], keyb[:], con[:, at:at + 1], None,
                                     ALU.is_equal).then_inc(S("permT"), 1)

                chooser(r * E)
                dve.wait_ge(S("key_bc"), r + 1)
                step(V_.tensor_copy(keyb[:], ps[:, 5, 0:N]))
                settle()
                chooser_T(r * E)
                for x in range(r * E, (r + 1) * E):
                    if x + 1 < (r + 1) * E:
                        chooser(x + 1)
                    dve.wait_ge(S("up"), 2 * x + 2)
                    if x >= 2:
                        dve.wait_ge(S("down"), x - 1)
                    for g in range(4, FG):
                        ins = V_.tensor_scalar(mid[:, x % 2, g, :], ps[:, 3, (g - 4) * CAP:(g - 3) * CAP],
                                               col("eb1", x % E * FG + g), 0.0, ALU.add, ALU.max)
                    ins.then_inc(S("mid_v"), 1)
                    if x + 1 < (r + 1) * E:
                        chooser_T(x + 1)
                    dve.wait_ge(S("down"), x + 1)
                    step(V_.tensor_copy(yhi[:, x % 2, :], ps[:, 4 + x % 2, 0:D]))
                    settle()
                    V_.tensor_tensor(ylo[:, x % 2, :], ps[:, 4 + x % 2, 0:D], yhi[:, x % 2, :].bitcast(F32),
                                     ALU.subtract).then_inc(S("y_parts"), 1)

            rounds(dve, experts)
            dve.wait_ge(S("residual"), 4)
            for h in range(2):
                dve.wait_ge(S("moe"), h + 1)
                V_.tensor_tensor(Y[:, 2 * h:2 * h + 2, :], ps[0:R, 6 + h, :].rearrange("p (i d) -> p i d", i=2),
                                 Y[:, 2 * h:2 * h + 2, :], ALU.add).then_inc(S("out_ready"), 2)

        @block.tensor
        def _(pe):
            mm = nc.tensor.matmul
            pe.wait_ge(S("ld_x"), 32)
            for j in range(NJ):
                mm(ps[:, j, :], w1[:, j, :], xw[:], start=True, stop=True).then_inc(S("conv1"), 1)
            pe.wait_ge(S("ld_w2"), 16)
            pe.wait_ge(S("h1"), NJ)
            for q in range(3):
                for s in range(2):
                    ins = mm(ps[:, 3 + q, :], w2[:, s, :], H1[:, 8 * q + s:8 * q + s + 8, :],
                             start=(s == 0), stop=(s == 1))
                ins.then_inc(S("conv2"), 1)
            pe.wait_ge(S("ld_w3"), 16)
            pe.wait_ge(S("h3_zeros"), 1)
            pe.wait_ge(S("h2"), 3)
            for m in range(KC):
                for k in range(5):
                    ins = mm(ps[:, 6 + m, 0:N], w3[:, k, m * P:(m + 1) * P], H2[:, 2 * k:2 * k + 21:S3, :],
                             start=(k == 0), stop=(k == 4))
                ins.then_inc(S("conv3"), 1)
            pe.wait_ge(S("ones"), 1)
            pe.wait_ge(S("w_sums"), 1)
            mm(ps[:, 4, 0:2], ones[:], wsum[:], start=True, stop=True).then_inc(S("w_total"), 1)

            pe.wait_ge(S("ld_w4"), 16)
            for m in range(KC):
                pe.wait_ge(S("h3"), m + 1)
                for k in range(3):
                    ins = mm(ps[:, m, 0:N], w4[:, m, k, :], H3[:, m, k:k + T, :], start=(k == 0), stop=(k == 2))
                ins.then_inc(S("conv4"), 1)
            pe.wait_ge(S("ld_w5"), 16)
            pe.wait_ge(S("h4"), 2)

            def token_major(bank, lhs, rhs, sem, nk=KC):
                for i in range(NT):
                    for k in range(nk):
                        ins = mm(ps[0:R, bank + i // 2, (i % 2) * D:(i % 2 + 1) * D],
                                 lhs(k, i), rhs(k), start=(k == 0), stop=(k == nk - 1))
                    if i % 2:
                        ins.then_inc(S(sem), 1)

            def awake(sem=None, value=0, products=AWAKE):
                if sem:
                    pe.wait_ge(S(sem), value)
                for _ in range(products):
                    mm(ps[:, 7, :], onesb[:], onesb[:].unsqueeze(1).to_broadcast([P, 4, P]), start=True, stop=True)

            def tile(x):
                return lambda k, i: x[:, k, i * R:(i + 1) * R]

            token_major(2, tile(H4), lambda k: w5[:, k, :], "conv5")

            def turn(src, tag, wait):
                pe.wait_ge(S("ld_con"), 16)
                for k in range(KC):
                    for i in range(NT):
                        if k == 0:
                            pe.wait_ge(S(wait), i + 1)
                        ins = nc.tensor.transpose(ps[:, k, i * R:(i + 1) * R], src[:, i, k * P:(k + 1) * P],
                                                  ident[0:R, 0:R])
                    ins.then_inc(S(tag), 1)

            for sem, value in (("h5", 1), ("roped", 1), ("roped", 2), ("squares", 1), ("rms_root", 1),
                               ("ln0_var", 1), ("ln0_root", 1)):
                awake(sem, value)
            turn(Z, "ln0_turned", "ln0_z")

            def attention(l, ln):
                pe.wait_ge(S(f"ld_a{l}"), 32)
                pe.wait_ge(S(ln + "_T"), 2)
                for t in range(T):
                    for k in range(KC):
                        for h in range(2):
                            ins = mm(ps[64 * h:64 * h + 64, t, 0:3 * P], ZT[:, k, t:N:T], wqkv[l][:, k, h, :],
                                     start=(k == 0), stop=(k == 1))
                    ins.then_inc(S("qkv"), 1)
                awake(products=4)
                awake("attending", 3 * l + 1)
                awake("attending", 3 * l + 2)
                if l:
                    awake("exp", l)
                awake("attending", 3 * l + 3)
                for i in range(T):
                    pe.wait_ge(S("weighted"), T * l + i + 1)
                    for j in range(T):
                        ins = mm(ps[:, 5 + i // 4, (i % 4) * P:(i % 4 + 1) * P], prod[:, i, j, :], ident,
                                 start=(j == 0), stop=(j == T - 1))
                    if i >= 3:
                        ins.then_inc(S("mixed"), 1)
                pe.wait_ge(S("mixed_T"), 2 * l + 2)
                token_major(0, tile(OT), lambda k: wo[l][:, k, :], "projected")

            attention(0, "ln0")

            pe.wait_ge(S("const_bf"), 1)
            awake(products=4)
            for sem, value in (("ln1_var", 1), ("ln1_root", 1), ("ln1_z", 1), ("ln1_z", NT), ("zq_scale", 1)):
                awake(sem, value)
            pe.wait_ge(S("zq"), 1)
            for k in range(KC):
                for i in range(NT):
                    ins = nc.tensor.transpose(ps[:, k, :].bitcast(BF16)[:, i * R:(i + 1) * R],
                                              Zq[:, i, k * P:(k + 1) * P], identb[0:R, 0:R])
                ins.then_inc(S("zq_turned"), 1)
            pe.wait_ge(S("iv1_diag"), 1)
            mm(ps[:, 2, 0:N], ones[0:R, :], diag[:], start=True, stop=True).then_inc(S("iv1_bc"), 1)
            pe.wait_ge(S("zq_T"), 2)
            pe.wait_ge(S("w_ternary"), 2)
            for g in range(FG):
                if g >= 5:
                    pe.wait_ge(S("hid_scaled"), g - 4)
                for k in range(KC):
                    ins = mm(ps[:, FFB[g], 0:N], f1q[:, k * FF + g * P:k * FF + (g + 1) * P], ZqT[:, k, :],
                             start=(k == 0), stop=(k == 1))
                ins.then_inc(S("ff1"), 1)
            pe.wait_ge(S("hid_scaled"), FG)
            for g in range(FG):
                awake("conv_done", g + 1)
            awake("silu", FG)
            awake("mx1", 1)
            for i in range(NT):
                ins = nc.tensor.transpose(ps[0:R, 0, i * P:(i + 1) * P], mx1[:, i * R:(i + 1) * R], ident)
            ins.then_inc(S("mx1_turned"), 1)
            awake("mx1_turned", 1)
            awake("qs2_diag", 1, 0)
            mm(ps[:, 1, 0:N], ones[0:R, :], diag[:], start=True, stop=True).then_inc(S("qs2_bc"), 1)
            for g in range(FG):
                pe.wait_ge(S("hq"), g + 1)
                for i in range(NT):
                    ins = mm(ps[0:R, 2 + i // 2, i % 2 * D:(i % 2 + 1) * D], hq[:, g, i * R:(i + 1) * R],
                             f2q[:, g * D:(g + 1) * D], start=(g == 0 and i % 2 == 0), stop=True,
                             skip_group_check=True)
                    if g == FG - 1 and i % 2:
                        ins.then_inc(S("ff2"), 1)

            awake(products=4)
            awake("ln2_var", 1)
            awake("ln2_root", 1)
            turn(Z, "ln2_turned", "ln2_z")
            attention(1, "ln2")
            awake(products=4)
            awake("ln3_var", 1)
            awake("ln3_root", 1)
            turn(Z, "ln3_turned", "ln3_z")
            attention(2, "ln3")

            awake(products=4)
            awake("ln4_var", 1)
            awake("ln4_root", 1)
            turn(Z, "ln4_turned", "ln4_z")
            pe.wait_ge(S("ld_gw"), 32)
            pe.wait_ge(S("ln4_T"), 2)
            for i in range(NT):
                for k in range(KC):
                    ins = mm(ps[0:R, 2, i * E:(i + 1) * E], ZT[:, k, i * R:(i + 1) * R], gw[:, k, :],
                             start=(k == 0), stop=(k == 1))
            ins.then_inc(S("logits"), 1)
            pe.wait_ge(S("onehot"), 1)
            for i in range(NT):
                ins = nc.tensor.transpose(ps[0:E, 3, i * R:(i + 1) * R], oh[:, i, :], ident[0:R, 0:R])
            ins.then_inc(S("oh_turned"), 1)
            for i in range(NT + 1):
                for j in range(min(i + 1, NT)):
                    ins = mm(ps[0:R, 4, i * E:(i + 1) * E], beforeb[:] if j == i else onesb[0:R, 0:R], ohb[:, j, :],
                             start=(j == 0), stop=(j == min(i, NT - 1)))
            ins.then_inc(S("ranks"), 1)

            def experts(r):
                pe.wait_ge(S("key_diag"), r + 1)
                if r:
                    pe.wait_ge(S("y_parts"), r * E)
                mm(ps[:, 5, 0:N], ones[0:R, :], diag[:], start=True, stop=True).then_inc(S("key_bc"), 1)

                def gather(x):
                    pe.wait_ge(S("perm"), x + 1)
                    if x >= 2:
                        pe.wait_ge(S("xe"), x - 1)
                    for k in range(KC):
                        for part, z in enumerate((zhi, zlo)):
                            for i in range(NT):
                                ins = mm(ps[:, x % 2, k * CAP:(k + 1) * CAP], z[:, i, k * P:(k + 1) * P],
                                         perm[:, x % 2, i, :], start=(part == 0 and i == 0),
                                         stop=(part == 1 and i == NT - 1))
                    ins.then_inc(S("gathered"), 1)

                def up(x):
                    pe.wait_ge(S(f"ld_e{x % RING}"), 32 * (x // RING + 1))
                    pe.wait_ge(S("xe"), x + 1)
                    for g in range(FG):
                        if x >= 1 and g % 4 == 0:
                            pe.wait_ge(S("mid_v" if g else "mid_a"), x)
                        for k in range(KC):
                            ins = mm(ps[:, 2 + g // 4, g % 4 * CAP:(g % 4 + 1) * CAP],
                                     ring1[:, x % RING, k, g * P:(g + 1) * P], xe[:, x % 2, k, :],
                                     start=(k == 0), stop=(k == 1))
                        if g % 4 == 3:
                            ins.then_inc(S("up"), 1)

                def down(x):
                    if x >= 2:
                        pe.wait_ge(S("y_parts"), x - 1)
                    for g in range(FG):
                        if g % 4 == 0:
                            pe.wait_ge(S("mid_v" if g else "mid_a"), x + 1)
                        ins = mm(ps[:, 4 + x % 2, 0:D], mid[:, x % 2, g, :], ring2[:, x % RING, g, :],
                                 start=(g == 0), stop=(g == FG - 1))
                    ins.then_inc(S("down"), 1)

                def scatter(x):
                    pe.wait_ge(S("permT"), x + 1)
                    pe.wait_ge(S("y_parts"), x + 1)
                    for i in range(NT):
                        for part, y in enumerate((yhi, ylo)):
                            ins = mm(ps[0:R, 6 + i // 2, i % 2 * D:(i % 2 + 1) * D],
                                     permT[:, x % 2, i * R:(i + 1) * R], y[:, x % 2, :],
                                     start=(x == 0 and i % 2 == 0 and part == 0), stop=True, skip_group_check=True)
                    ins.then_inc(S("scattered"), 1)

                if r == 0:
                    pe.wait_ge(S("z_parts"), 1)
                gather(r * E)
                for x in range(r * E, (r + 1) * E):
                    up(x)
                    if x + 1 < (r + 1) * E:
                        gather(x + 1)
                    if x > r * E:
                        scatter(x - 1)
                    down(x)
                scatter((r + 1) * E - 1)

            pe.wait_ge(S("oh_T"), 1)
            rounds(pe, experts)
            for i in range(NT):
                ins = mm(ps[0:R, 6 + i // 2, i % 2 * D:(i % 2 + 1) * D], ohT[:, i * R:(i + 1) * R], eb2[:],
                         start=False, stop=True, skip_group_check=True)
                if i % 2:
                    ins.then_inc(S("moe"), 1)


def _turned(w):
    o, i = w.shape
    return np.ascontiguousarray(w.T.reshape(i // P, P, o).transpose(1, 0, 2))


def _halves(v):
    return v.reshape(-1, P).T


def _layout(x):
    f = {k: np.asarray(v) for k, v in x.items()}
    a = {}
    xp = np.zeros((B, WIN * (NG - 1) + P), np.float32)
    xp[:, K1 // 2:K1 // 2 + L] = f["x"][:, 0, :]
    a["xw"] = np.stack([xp[:, WIN * g:WIN * g + P].T for g in range(NG)], 1)
    w = np.zeros((P, NJ, TM, C1), np.float32)
    for j in range(NJ):
        for t in range(TM):
            s = (j * TM + t) * S1
            w[s:s + K1, j, t, :] = f["L0_tok_w1"][:, 0, :].T
    a["w1"] = w.reshape(P, NJ, P)
    w = np.zeros((TM, C1, 2, 2, C2), np.float32)
    for t in range(TM):
        for s in range(2):
            k = t + 4 * s - 1
            if k >= 0:
                w[t, :, s, :, :] = f["L0_tok_w2"][:, :, k].T[:, None, :]
    a["w2"] = w.reshape(P, 2, P)
    w = np.zeros((2, C2, 5, D), np.float32)
    for k in range(K3):
        w[k % 2, :, k // 2, :] = f["L0_tok_w3"][:, :, k].T
    a["w3"] = w.reshape(P, 5, D)
    w = np.zeros((P, KC, 3, P), np.float32)
    for g in range(D // 8):
        m, c = g // 16, (g % 16) * 8
        w[c:c + 8, m, :, c:c + 8] = f["L0_tok_w4"][g * 8:g * 8 + 8].transpose(1, 2, 0)
    a["w4"] = w
    a["w5"] = _turned(f["L0_tok_w5"][:, :, 0])
    by_head = np.arange(D).reshape(D // HA, HA).T.ravel()
    a0 = f["L0_attn_w_qkv"].reshape(3, D, D)[:, by_head]
    b0 = f["L0_attn_b_qkv"].reshape(3, D)[:, by_head]
    qkv = [a0, np.stack([f["L1_attn_W" + c] for c in "qkv"]), np.stack([f["L1_ffn_w" + c].T for c in "qkv"])]
    bias = [b0, np.stack([f["L1_attn_b" + c] for c in "qkv"]), np.stack([f["L1_ffn_b" + c] for c in "qkv"])]
    for l in range(3):
        a[f"wqkv{l}"] = qkv[l].reshape(3, 2, P, KC, P).transpose(4, 3, 1, 0, 2).reshape(P, KC, 2, 3 * P)
    a["bqkv"] = np.stack(bias).reshape(3, 3, 2, P).transpose(2, 0, 1, 3).reshape(2, 3, 3 * P)
    a["wo0"] = _turned(f["L0_attn_w_o"])
    a["wo1"] = _turned(f["L1_attn_Wo"])
    a["wo2"] = _turned(f["L1_ffn_wo"].T)
    a["f1"] = _turned(f["L0_ffn_w1"]).reshape(P, -1)
    a["f2"] = _turned(f["L0_ffn_w2"]).reshape(P, -1)
    a["gw"] = _turned(f["L1_ffn_gate_w"].T)
    a["e1"] = np.ascontiguousarray(f["L1_ffn_w1"].reshape(E, KC, P, FF).transpose(0, 2, 1, 3))
    a["e2"] = np.ascontiguousarray(f["L1_ffn_w2"].reshape(E, FG, P, D).transpose(0, 2, 1, 3))
    a["eb2"] = f["L1_ffn_b2"]
    c = {
        "b1": np.tile(f["L0_tok_b1"], TM)[:, None], "b2": np.tile(f["L0_tok_b2"], 2)[:, None],
        "b3": _halves(f["L0_tok_b3"]), "b4": _halves(f["L0_tok_b4"]),
        "cw": f["L0_ffn_conv_w"].reshape(FG, P, 3).transpose(1, 0, 2).reshape(P, 24),
        "cb": _halves(f["L0_ffn_conv_b"]),
        "g1": _halves(f["L1_ffn_ln1_g"]), "h1": _halves(f["L1_ffn_ln1_b"]),
        "g2": _halves(f["L1_ffn_ln2_g"]), "h2": _halves(f["L1_ffn_ln2_b"]),
        "eb1": _halves(f["L1_ffn_b1"]),
    }
    a["cols"] = np.concatenate([c[n] for n, _ in COLS], 1)
    r = {"b5": f["L0_tok_b5"], "nw": f["L0_tok_norm_w"], "bo0": f["L0_attn_b_o"],
         "bo1": f["L1_attn_bo"], "bo2": f["L1_ffn_bo"],
         "gb": f["L1_ffn_gate_b"], "fr": f["L0_tok_rope_freqs"]}
    a["rows"] = np.concatenate([r[n] for n, _ in ROWS])
    p = np.arange(P)
    con = {
        "ident": np.eye(P),
        "before": (p[:, None] < np.arange(R)) * 1.0,
        "slot": p[:, None] + CAP * np.arange(E) * 1.0,
        "slots": np.tile(np.arange(E * CAP), (P, 1)) * 1.0,
        "tpos": (p % T)[:, None] * 1.0, "rank": np.tile(E - np.arange(E), (P, 1)) * 1.0,
    }
    a["con"] = np.concatenate([con[n] for n, _ in CONST], 1).astype(np.float32)
    return {k: np.ascontiguousarray(v) for k, v in a.items()}


def kernel(**inputs):
    import concourse.bacc as _bacc
    from concourse import mybir as _mybir
    from concourse.bass_utils import run_bass_kernel_spmd as _run

    nc = _bacc.Bacc("TRN2", target_bir_lowering=False, num_devices=1)
    arrays, aps = {}, {}
    for name, v in _layout(inputs).items():
        arrays[f"in_{name}"] = v
        aps[name] = nc.dram_tensor(f"in_{name}", v.shape, _mybir.dt.from_np(v.dtype), kind="ExternalInput").ap()
    out = nc.dram_tensor("out", (B, T, D), F32, kind="ExternalOutput").ap()
    tower(nc, aps, out)
    r = _run(nc, [arrays], core_ids=[0])
    return r.results[0]["out"]
```
